# Optimizing a Trainium2 kernel written in Bass

```python
import numpy as np
import jax
import jax.numpy as jnp

def _softmax(x, axis=-1):
    return jax.nn.softmax(x, axis=axis)

def _gelu(x):
    return jax.nn.gelu(x, approximate=True)

def _silu(x):
    return jax.nn.silu(x)

def _sigmoid(x):
    return jax.nn.sigmoid(x)

def _layernorm(x, axis=-1, eps=1e-05):
    m = jnp.mean(x, axis=axis, keepdims=True)
    v = jnp.var(x, axis=axis, keepdims=True)
    return (x - m) / jnp.sqrt(v + eps)

def _scatter_add(tgt, idx, src, axis=0):
    return tgt.at[idx].add(src)

def _segment_sum(src, seg, n):
    return jax.ops.segment_sum(src, seg, n)
kernel_name = 'mk_audio_tower_d1_tok_audfeat256_r4_6cf3d0'

def setup_inputs(seed: int=0):
    np.random.seed(seed)
    _w = jnp.asarray

    def _rec_inputs():
        import jax
        import jax.numpy as jnp
        _rk = jax.random.key(seed)
        x = -0.000392918 + 0.999932 * jax.random.normal(jax.random.fold_in(_rk, 1), (64, 375, 16), jnp.float32)
        return x
    x = _rec_inputs()

    def _L0_tok_setup():
        import jax, jax.numpy as jnp
        import numpy as np
        PATCH = 16
        STRIDE = 8
        EPS = 1e-05
        key = jax.random.key(seed)
        k1, k2, k3 = jax.random.split(key, 3)
        B, S, F, D = (128, 2048, 16, 64)
        in_dim = F * PATCH
        x = jax.random.normal(k1, (B, S, F), dtype=jnp.float32)
        bound = 1.0 / np.sqrt(in_dim)
        W = jax.random.uniform(k2, (D, in_dim), minval=-bound, maxval=bound, dtype=jnp.float32)
        b = jax.random.uniform(k3, (D,), minval=-bound, maxval=bound, dtype=jnp.float32)
        gamma = jnp.ones((D,), dtype=jnp.float32)
        beta = jnp.zeros((D,), dtype=jnp.float32)
        return {'x': x, 'W': W, 'b': b, 'gamma': gamma, 'beta': beta}
    _L0_tok_all = _L0_tok_setup()
    _L0_tok_in = {k: v for k, v in _L0_tok_all.items() if k in ('W', 'b', 'gamma', 'beta')}
    del _L0_tok_all

    def _L0_attn_setup():
        import jax, jax.numpy as jnp
        import numpy as np
        key = jax.random.key(seed)
        k1, k2, k3 = jax.random.split(key, 3)
        b, n_t, n, n_h = (8, 256, 64, 8)
        s = jax.random.normal(k1, (b, n_t, n), dtype=jnp.float32)
        Q = jax.random.normal(k2, (n_h, n, n), dtype=jnp.float32) * 0.02
        E = jax.random.normal(k3, (n_h, n, n), dtype=jnp.float32) * 0.02
        return {'s': s, 'Q': Q, 'E': E}
    _L0_attn_all = _L0_attn_setup()
    _L0_attn_in = {k: v for k, v in _L0_attn_all.items() if k in ('Q', 'E')}
    del _L0_attn_all

    def _L0_ffn_setup():
        import jax, jax.numpy as jnp
        import numpy as np
        E, D, H, TOP_K = (6, 64, 64, 2)
        ROUTER_H = D // 2
        key = jax.random.key(seed)
        ks = jax.random.split(key, 12)
        s = 1.0 / np.sqrt(D)
        sh = 1.0 / np.sqrt(H)
        sr = 1.0 / np.sqrt(ROUTER_H)
        return {'features': jax.random.normal(ks[0], (8, 1024, D), dtype=jnp.float32), 'router_w1': jax.random.uniform(ks[1], (D, ROUTER_H), jnp.float32, -s, s), 'router_b1': jnp.zeros((ROUTER_H,), jnp.float32), 'router_w2': jax.random.uniform(ks[2], (ROUTER_H, E), jnp.float32, -sr, sr), 'router_b2': jnp.zeros((E,), jnp.float32), 'expert_w1': jax.random.uniform(ks[3], (E, D, H), jnp.float32, -s, s), 'expert_b1': jnp.zeros((E, H), jnp.float32), 'expert_w2': jax.random.uniform(ks[4], (E, H, H), jnp.float32, -sh, sh), 'expert_b2': jnp.zeros((E, H), jnp.float32), 'expert_w3': jax.random.uniform(ks[5], (E, H, D), jnp.float32, -sh, sh), 'expert_b3': jnp.zeros((E, D), jnp.float32)}
    _L0_ffn_all = _L0_ffn_setup()
    _L0_ffn_in = {k: v for k, v in _L0_ffn_all.items() if k in ('router_w1', 'router_b1', 'router_w2', 'router_b2', 'expert_w1', 'expert_b1', 'expert_w2', 'expert_b2', 'expert_w3', 'expert_b3')}
    del _L0_ffn_all
    return {'x': x, 'L0_tok_W': _L0_tok_in['W'], 'L0_tok_b': _L0_tok_in['b'], 'L0_tok_gamma': _L0_tok_in['gamma'], 'L0_tok_beta': _L0_tok_in['beta'], 'L0_attn_Q': _L0_attn_in['Q'], 'L0_attn_E': _L0_attn_in['E'], 'L0_ffn_router_w1': _L0_ffn_in['router_w1'], 'L0_ffn_router_b1': _L0_ffn_in['router_b1'], 'L0_ffn_router_w2': _L0_ffn_in['router_w2'], 'L0_ffn_router_b2': _L0_ffn_in['router_b2'], 'L0_ffn_expert_w1': _L0_ffn_in['expert_w1'], 'L0_ffn_expert_b1': _L0_ffn_in['expert_b1'], 'L0_ffn_expert_w2': _L0_ffn_in['expert_w2'], 'L0_ffn_expert_b2': _L0_ffn_in['expert_b2'], 'L0_ffn_expert_w3': _L0_ffn_in['expert_w3'], 'L0_ffn_expert_b3': _L0_ffn_in['expert_b3']}

def reference(x, L0_tok_W, L0_tok_b, L0_tok_gamma, L0_tok_beta, L0_attn_Q, L0_attn_E, L0_ffn_router_w1, L0_ffn_router_b1, L0_ffn_router_w2, L0_ffn_router_b2, L0_ffn_expert_w1, L0_ffn_expert_b1, L0_ffn_expert_w2, L0_ffn_expert_b2, L0_ffn_expert_w3, L0_ffn_expert_b3):
    import jax
    import jax.numpy as jnp

    def _L0_tok_ref(x, W, b, gamma, beta):
        import jax, jax.numpy as jnp
        import numpy as np
        PATCH = 16
        STRIDE = 8
        EPS = 1e-05
        B, S, F = x.shape
        starts = jnp.arange(0, S - PATCH + 1, STRIDE)
        idx = starts[:, None] + jnp.arange(PATCH)[None, :]
        patches = x[:, idx, :].reshape(B, idx.shape[0], PATCH * F)
        y = jnp.einsum('bpi,di->bpd', patches, W) + b
        mu = jnp.mean(y, axis=-1, keepdims=True)
        var = jnp.mean(jnp.square(y - mu), axis=-1, keepdims=True)
        return (y - mu) * jax.lax.rsqrt(var + EPS) * gamma + beta

    def _L0_attn_ref(s, Q, E):
        import jax, jax.numpy as jnp
        import numpy as np
        n_t = s.shape[1]
        qs = jnp.einsum('bti,hij->bhtj', s, Q)
        Omega = jnp.einsum('bhtj,buj->bhtu', qs, s)
        mask = jnp.tril(jnp.ones((n_t, n_t), dtype=s.dtype))
        Omega = Omega * mask
        es = jnp.einsum('hij,buj->bhui', E, s)
        r = jnp.einsum('bhtu,bhui->bti', Omega, es)
        return r

    def _L0_ffn_ref(features, router_w1, router_b1, router_w2, router_b2, expert_w1, expert_b1, expert_w2, expert_b2, expert_w3, expert_b3):
        import jax, jax.numpy as jnp
        import numpy as np
        E, D, H, TOP_K = (6, 64, 64, 2)
        ROUTER_H = D // 2
        rh = jax.nn.relu(features @ router_w1 + router_b1)
        expert_logits = jax.nn.softmax(rh @ router_w2 + router_b2, axis=-1)
        top_w, top_i = jax.lax.top_k(expert_logits, TOP_K)
        routing_weights = jax.nn.softmax(top_w, axis=-1)
        h1 = jax.nn.relu(jnp.einsum('bsd,edh->bseh', features, expert_w1) + expert_b1)
        h2 = jax.nn.relu(jnp.einsum('bseh,ehf->bsef', h1, expert_w2) + expert_b2)
        expert_out = jnp.einsum('bsef,efo->bseo', h2, expert_w3) + expert_b3
        sel = jnp.take_along_axis(expert_out, top_i[:, :, :, None], axis=2)
        combined = jnp.sum(sel * routing_weights[..., None], axis=2)
        return combined
    h = _L0_tok_ref(x, L0_tok_W, L0_tok_b, L0_tok_gamma, L0_tok_beta)
    h = h + _L0_attn_ref(_layernorm(h, axis=-1), L0_attn_Q, L0_attn_E)
    h = h + _L0_ffn_ref(_layernorm(h, axis=-1), L0_ffn_router_w1, L0_ffn_router_b1, L0_ffn_router_w2, L0_ffn_router_b2, L0_ffn_expert_w1, L0_ffn_expert_b1, L0_ffn_expert_w2, L0_ffn_expert_b2, L0_ffn_expert_w3, L0_ffn_expert_b3)
    return h

_drawn_inputs = setup_inputs


def setup_inputs(seed=0):
    import zlib

    import numpy as np

    out = dict(_drawn_inputs(seed))
    spreads = {'L0_tok_gamma': (1.0, 0.2),
     'L0_tok_beta': (0.0, 0.1),
     'L0_ffn_router_b1': (0.0, 0.685),
     'L0_ffn_router_b2': (0.0, 0.484),
     'L0_ffn_expert_b1': (0.0, 0.8),
     'L0_ffn_expert_b2': (0.0, 0.8),
     'L0_ffn_expert_b3': (0.0, 0.456)}
    factors = {'L0_ffn_expert_w1': 4.057, 'L0_ffn_expert_w2': 3.536, 'L0_ffn_expert_w3': 2.748}
    for name, (base, spread) in spreads.items():
        noise = np.random.default_rng([zlib.crc32(name.encode()), seed]).standard_normal(out[name].shape)
        drawn = base * np.exp(spread * noise) if base else spread * noise
        out[name] = jnp.asarray(drawn.astype(out[name].dtype))
    for name, factor in factors.items():
        out[name] = (out[name] * factor).astype(out[name].dtype)
    return out
```

```python
import concourse.bass as bass
from concourse import mybir
from contextlib import ExitStack



def audio_tower(nc, x, tok_w, tok_b, tok_gamma, tok_beta, attn_q, attn_e, router_w1, router_b1,
                router_w2, router_b2, w1, b1, w2, b2, w3, b3, out):
    F32, F32R = mybir.dt.float32, mybir.dt.float32r
    ALU, ACT, AX = mybir.AluOpType, mybir.ActivationFunctionType, mybir.AxisListType

    CLIPS, STEPS, FREQ = x.shape
    D, PATCH_IN = tok_w.shape
    HEADS = attn_q.shape[0]
    EXPERTS, _, HID = w1.shape
    RHID = router_w1.shape[1]
    T = out.shape[1]
    EPS = 1e-5
    BLK = PATCH_IN // 2
    NBLK = T + 1
    GC = 8
    GP = GC // 2
    G = CLIPS // GC
    N = GC * T
    ROWS = 64 + T
    BROWS = 64 + NBLK
    HP = HEADS // 2
    EP = EXPERTS // 2
    XCOLS = NBLK * BLK

    x_blocks = x.rearrange("b r f -> b (r f)")[:, 0:XCOLS].rearrange(
        "(p side) (k c) -> side k p c", side=2, c=BLK)
    out_rows = out.rearrange("(p side) t d -> side t p d", side=2)

    with ExitStack() as ctx:
        def sb(name, shape, dt=F32):
            return ctx.enter_context(nc.sbuf_tensor(name, shape, dt))

        def pb(name):
            return ctx.enter_context(nc.psum_tensor(name, [128, 512], F32))

        def sem(name):
            return ctx.enter_context(nc.semaphore(name))

        ident = sb("ident", [128, 128])
        causal = sb("causal", [128, N])
        earlier = sb("earlier", [128, EXPERTS, EXPERTS])
        minus_half = sb("minus_half", [128, GP])
        eps_sb = sb("eps_sb", [128, GP])
        q_raw = sb("q_raw", [128, HP, 128])
        q_hi = sb("q_hi", [128, HP, 128], F32R)
        q_lo = sb("q_lo", [128, HP, 128], F32R)
        w1_raw = sb("w1_raw", [128, EP, 128])
        w1_hi = sb("w1_hi", [128, EP, 128], F32R)
        w1_lo = sb("w1_lo", [128, EP, 128], F32R)
        rw1_raw = sb("rw1_raw", [128, RHID])
        rw1_hi = sb("rw1_hi", [128, RHID], F32R)
        rw1_lo = sb("rw1_lo", [128, RHID], F32R)
        e_raw = sb("e_raw", [D, HEADS * D])
        tokw_raw = sb("tokw_raw", [D, PATCH_IN])
        e_t = sb("e_t", [128, HP, D])
        tokw_t = sb("tokw_t", [128, 2, D])
        w2_diag = sb("w2_diag", [128, EP, 128])
        w3_sb = sb("w3_sb", [128, EP, D])
        rw2_sb = sb("rw2_sb", [RHID, EXPERTS])
        b1_sb = sb("b1_sb", [128, EP])
        b2_sb = sb("b2_sb", [128, EP])
        rb1_sb = sb("rb1_sb", [RHID, 1])
        b3_raw = sb("b3_raw", [128, GP, D])
        b3_hi = sb("b3_hi", [128, GP, D], F32R)
        b3_lo = sb("b3_lo", [128, GP, D], F32R)
        spread_raw = sb("spread_raw", [128, GP * EP * 128])
        spread = sb("spread", [128, GP, EP, 128], F32R)
        tokb_sb = sb("tokb_sb", [128, D])
        gamma_sb = sb("gamma_sb", [128, D])
        beta_sb = sb("beta_sb", [128, D])
        rb2_sb = sb("rb2_sb", [128, EXPERTS])

        xin = sb("xin", [128, GP, BLK])
        x_t = sb("x_t", [128, GP, BROWS])
        y = sb("y", [128, GP, D])
        y_c = sb("y_c", [128, GP, D])
        y_sq = sb("y_sq", [128, GP, D])
        y_n = sb("y_n", [128, GP, D])
        y_g = sb("y_g", [128, GP, D])
        hbuf = sb("hbuf", [128, G, GP, D])
        h_c = sb("h_c", [128, GP, D])
        h_sq = sb("h_sq", [128, GP, D])
        h = sb("h", [128, GP, D])
        s = sb("s", [128, GP + 1, D])
        st1 = sb("st1", [128, 4, GP])
        st2 = sb("st2", [128, 4, GP])
        st3 = sb("st3", [128, 4, GP])

        s_split = sb("s_split", [128, GC, T], F32R)
        s_feat = sb("s_feat", [128, GC, 128])
        s_tok = sb("s_tok", [128, GC, 128])
        qs = sb("qs", [128, GC, HP, T])
        omega = sb("omega", [128, GC, HP, T])
        z_t = sb("z_t", [128, HP, GP, 128])
        a_c = sb("a_c", [128, GP, D])
        a_sq = sb("a_sq", [128, GP, D])
        a = sb("a", [128, GP, D])
        a_n = sb("a_n", [128, GP + 1, D])

        h_split = sb("h_split", [128, GC, T], F32R)
        rh = sb("rh", [RHID, GC, 64])
        logits = sb("logits", [128, GP, EXPERTS])
        logits_c = sb("logits_c", [128, GP, EXPERTS])
        ex = sb("ex", [128, GP, EXPERTS])
        probs = sb("probs", [128, GP, EXPERTS])
        ex2 = sb("ex2", [128, GP, EXPERTS])
        picked = sb("picked", [128, GP, EXPERTS])
        rank = sb("rank", [128, GP, EXPERTS])
        above = sb("above", [128, GP, EXPERTS, EXPERTS])
        tied = sb("tied", [128, GP, EXPERTS, EXPERTS])
        tied_e = sb("tied_e", [128, GP, EXPERTS, EXPERTS])
        beats = sb("beats", [128, GP, EXPERTS, EXPERTS])
        rst = sb("rst", [128, 5, GP])
        gate = sb("gate", [128, GP, EXPERTS])
        gate_parts = sb("gate_parts", [128, 128])
        gate_t = sb("gate_t", [128, 128], F32R)
        h1 = sb("h1", [128, EP, N])
        h2 = sb("h2", [128, EP, N])
        h2w = sb("h2w", [128, EP, GC, 64])
        GATES = GP * EXPERTS
        gate_up = gate_parts[:, 0:GATES].rearrange("p (a e) -> p a e", a=GP)
        gate_low = gate_parts[:, GATES:2 * GATES].rearrange("p (a e) -> p a e", a=GP)

        ring = [pb("ring0"), pb("ring1")]
        om = [pb("om0"), pb("om1")]
        zb = [pb("zb0"), pb("zb1")]
        tb = pb("tb")
        yb = pb("yb")

        def pairs_of(bank, width):
            return bank[:, :].rearrange("p (a c) -> p a c", a=GP)[:, :, 0:width]

        def clips_of(bank):
            return bank[:, :].rearrange("p (c u) -> p c u", u=64)[:, :, 0:T]

        y_ps = yb[:, 0:GP * D].rearrange("p (a d) -> p a d", a=GP)
        l_ps = yb[:, 0:GP * EXPERTS].rearrange("p (a e) -> p a e", a=GP)

        x_loaded, stored = sem("x_loaded"), sem("stored")
        tokw_loaded, q_loaded, e_loaded, rows_loaded, rest_loaded = (
            sem(n) for n in ("tokw_loaded", "q_loaded", "e_loaded", "rows_loaded", "rest_loaded"))
        xin_cleared, cleared, consts = sem("xin_cleared"), sem("cleared"), sem("consts")
        half_mask, mask_made = sem("half_mask"), sem("mask_made")
        pool_step = sem("pool_step")
        e_in_psum, e_copied = sem("e_in_psum"), sem("e_copied")
        w_in_psum, w_copied, q_rounded, q_split = (
            sem(n) for n in ("w_in_psum", "w_copied", "q_rounded", "q_split"))
        x_in_psum, x_copied, y_in_psum = sem("x_in_psum"), sem("x_copied"), sem("y_in_psum")
        y_added, y_summed, y_centred, y_squared, y_var = (
            sem(n) for n in ("y_added", "y_summed", "y_centred", "y_squared", "y_var"))
        y_veps, y_rstd, y_normed, y_scaled, h_ready = (
            sem(n) for n in ("y_veps", "y_rstd", "y_normed", "y_scaled", "h_ready"))
        h_summed, h_centred, h_squared, h_var, h_veps, h_rstd, s_ready = (
            sem(n) for n in ("h_summed", "h_centred", "h_squared", "h_var", "h_veps", "h_rstd", "s_ready"))
        s_in_psum, s_upper, s_feat_top, s_feat_made, s_split_made, s_tok_made = (
            sem(n) for n in ("s_in_psum", "s_upper", "s_feat_top", "s_feat_made", "s_split_made", "s_tok_made"))
        qs_in_psum = [sem(f"qs_in_psum{i}") for i in range(HP)]
        qs_copied = [sem(f"qs_copied{i}") for i in range(HP)]
        om_in_psum = [sem(f"om_in_psum{i}") for i in range(GP)]
        om_masked = [sem(f"om_masked{i}") for i in range(GP)]
        z_in_psum = [sem(f"z_in_psum{i}") for i in range(GP)]
        z_copied = [sem(f"z_copied{i}") for i in range(GP)]
        r_in_psum, a_ready, a_summed, a_centred, a_squared, a_var, a_veps, a_rstd, a_normed = (
            sem(n) for n in ("r_in_psum", "a_ready", "a_summed", "a_centred", "a_squared", "a_var",
                             "a_veps", "a_rstd", "a_normed"))
        h_kept, a_kept = sem("h_kept"), sem("a_kept")
        a_in_psum, a_upper, a_split_made = sem("a_in_psum"), sem("a_upper"), sem("a_split_made")
        rh_in_psum, rh_made, l_in_psum, l_added, l_max, l_centred, ex_made = (
            sem(n) for n in ("rh_in_psum", "rh_made", "l_in_psum", "l_added", "l_max", "l_centred", "ex_made"))
        ex_summed, ex_inv, probs_made, ex2_made, above_made, tied_made, tied_cut, beats_made = (
            sem(n) for n in ("ex_summed", "ex_inv", "probs_made", "ex2_made", "above_made", "tied_made",
                             "tied_cut", "beats_made"))
        rank_made, picked_made, picked_sum, picked_inv, gate_made, gate_upper, gate_split = (
            sem(n) for n in ("rank_made", "picked_made", "picked_sum", "picked_inv", "gate_made",
                             "gate_upper", "gate_split"))
        spread_made, spread_rounded = sem("spread_made"), sem("spread_rounded")
        h1_in_psum = [sem(f"h1_in_psum{i}") for i in range(EP)]
        h1_made = [sem(f"h1_made{i}") for i in range(EP)]
        gate_in_psum = [sem(f"gate_in_psum{i}") for i in range(EP)]
        h2_in_psum = [sem(f"h2_in_psum{i}") for i in range(EP)]
        h2_made = [sem(f"h2_made{i}") for i in range(EP)]
        h2_weighted = [sem(f"h2_weighted{i}") for i in range(EP)]
        gt_in_psum, gt_copied, o_in_psum, o_added = (
            sem(n) for n in ("gt_in_psum", "gt_copied", "o_in_psum", "o_added"))

        block = ctx.enter_context(nc.Block())

        def counts(engine, g):
            if isinstance(g, int):
                return g + 2, g + 1, g, g - 1
            return engine.snap(g + 2), engine.snap(g + 1), g, engine.snap(g - 1)

        def turns(engine, turn):
            turn(-1, project=True, attend=False, experts=False)
            turn(0, project=True, attend=True, experts=False)
            turn(1, project=True, attend=True, experts=True)
            with engine.Fori(2, G - 2) as g:
                turn(g, project=True, attend=True, experts=True)
            turn(G - 2, project=True, attend=True, experts=True)
            turn(G - 1, project=False, attend=True, experts=True)
            turn(G, project=False, attend=False, experts=True)

        def since(g, first):
            return not isinstance(g, int) or g >= first

        @block.sync
        def _(sp):
            sp.wait_ge(xin_cleared, 1)

            def load_blocks(group):
                for side in range(2):
                    sp.dma_start(xin[64 * side:64 * side + NBLK, :, :],
                                 x_blocks[side][:, bass.ds(group * GP, GP), :]).then_inc(x_loaded, 16)

            load_blocks(0)
            for half in range(2):
                sp.dma_start(q_raw[64 * half:64 * half + D, :, :].rearrange("i p (s j) -> i (p s) j", s=2),
                             attn_q.rearrange("h i j -> i h j")).then_inc(q_loaded, 16)
            for half in range(2):
                rows = slice(64 * half, 64 * half + D)
                sp.dma_start(rw1_raw[rows, :], router_w1).then_inc(q_loaded, 16)
                sp.dma_start(w1_raw[rows, :, :].rearrange("d p (s h) -> d (p s) h", s=2),
                             w1.rearrange("e d h -> d e h")).then_inc(q_loaded, 16)
            sp.dma_start(rb1_sb[:], router_b1.unsqueeze(1)).then_inc(rest_loaded, 16)
            sp.dma_start(rw2_sb[:], router_w2).then_inc(rest_loaded, 16)
            sp.dma_start(b1_sb[:], b1.rearrange("(p s) h -> (s h) p", s=2),
                         allow_slow_non_contiguous=True).then_inc(rest_loaded, 16)
            sp.dma_start(b2_sb[:], b2.rearrange("(p s) h -> (s h) p", s=2),
                         allow_slow_non_contiguous=True).then_inc(rest_loaded, 16)
            sp.dma_start(w3_sb[:], w3.rearrange("(p s) f o -> (s f) p o", s=2)).then_inc(rest_loaded, 16)
            sp.wait_ge(cleared, 10)
            for half in range(2):
                rows = slice(64 * half, 64 * half + HID)
                sp.dma_start(w2_diag[rows, :, rows],
                             w2.rearrange("(p s) h f -> s h p f", s=2)[half]).then_inc(rest_loaded, 16)
            for p in range(GP):
                for top in (EXPERTS * p, EXPERTS * (GP + p)):
                    sp.dma_start(b3_raw[top:top + EXPERTS, p, :], b3).then_inc(rest_loaded, 16)

            def turn(g, project, attend, experts):
                ahead, now, last, before = counts(sp, g)
                if project and not (isinstance(g, int) and g == G - 2):
                    sp.wait_ge(x_in_psum, ahead)
                    load_blocks(g + 2)
                if experts:
                    sp.wait_ge(o_added, last)
                    for side in range(2):
                        sp.dma_start(out_rows[side][:, bass.ds(g * GP - GP, GP), :],
                                     hbuf[64 * side:64 * side + T, bass.ds(g - 1, 1), :, :].rearrange(
                                         "p g a d -> p (g a) d")).then_inc(stored, 16)

            turns(sp, turn)
            sp.wait_ge(stored, 32 * G)

        @block.gpsimd
        def _(pool):
            eng = nc.gpsimd
            eng.memset(ident[:], 0.0).then_inc(pool_step, 1)
            pool.wait_ge(pool_step, 1)
            eng.affine_select(out=ident[:], in_=ident[:], compare_op=ALU.not_equal, fill=1.0, base=0,
                              pattern=[[-1, 128]], channel_multiplier=1).then_inc(consts, 1)
            eng.memset(minus_half[:], -0.5).then_inc(pool_step, 1)
            eng.memset(eps_sb[:], EPS).then_inc(pool_step, 1)
            eng.memset(earlier[:], 1.0).then_inc(pool_step, 1)
            eng.memset(causal[:], 1.0).then_inc(pool_step, 1)
            pool.wait_ge(pool_step, 5)
            eng.affine_select(out=causal[0:64, :].rearrange("p (c t) -> p c t", c=GC),
                              in_=causal[0:64, :].rearrange("p (c t) -> p c t", c=GC),
                              compare_op=ALU.is_ge, fill=0.0, base=0, pattern=[[0, GC], [1, T]],
                              channel_multiplier=-1).then_inc(half_mask, 1)
            eng.affine_select(out=earlier[:], in_=earlier[:], compare_op=ALU.is_gt, fill=0.0, base=0,
                              pattern=[[1, EXPERTS], [-1, EXPERTS]], channel_multiplier=0).then_inc(consts, 1)
            eng.memset(spread_raw[:], 0.0).then_inc(pool_step, 1)
            for part in range(2):
                pool.wait_ge(pool_step, 6 + part)
                done = eng.affine_select(out=spread_raw[:], in_=spread_raw[:], compare_op=ALU.not_equal, fill=1.0,
                                         base=-GATES * part,
                                         pattern=[[-EXPERTS, GP], [-2, EP], [-1, 2], [0, HID]], channel_multiplier=1)
                done.then_inc(pool_step if part == 0 else spread_made, 1)
            eng.memset(s_tok[:], 0.0).then_inc(cleared, 1)
            eng.memset(z_t[:], 0.0).then_inc(cleared, 1)
            eng.memset(h2w[:], 0.0).then_inc(cleared, 1)

            def rstd(st, var, veps, rstd_, value):
                pool.wait_ge(var, value)
                eng.tensor_tensor(st[0:ROWS, 2, :], st[0:ROWS, 1, :], eps_sb[0:ROWS, :], ALU.add).then_inc(veps, 1)
                pool.wait_ge(veps, value)
                eng.tensor_tensor(st[0:ROWS, 3, :], st[0:ROWS, 2, :], minus_half[0:ROWS, :],
                                  ALU.pow).then_inc(rstd_, 1)
                pool.wait_ge(rstd_, value)

            def wide(v):
                return v.unsqueeze(2).to_broadcast([ROWS, GP, D])

            def row(v):
                return v.unsqueeze(1).to_broadcast([ROWS, GP, D])

            pool.wait_ge(rows_loaded, 64)
            pool.wait_ge(cleared, 10)

            def turn(g, project, attend, experts):
                ahead, now, last, before = counts(pool, g)
                if project:
                    rstd(st1, y_var, y_veps, y_rstd, ahead)
                    eng.tensor_tensor(y_n[0:ROWS], y_c[0:ROWS], wide(st1[0:ROWS, 3, :]),
                                      ALU.mult).then_inc(y_normed, 1)
                    pool.wait_ge(y_normed, ahead)
                    eng.tensor_tensor(y_g[0:ROWS], y_n[0:ROWS], row(gamma_sb[0:ROWS, :]),
                                      ALU.mult).then_inc(y_scaled, 1)
                    pool.wait_ge(y_scaled, ahead)
                    eng.tensor_tensor(h[0:ROWS], y_g[0:ROWS], row(beta_sb[0:ROWS, :]), ALU.add).then_inc(h_ready, 1)
                    rstd(st2, h_var, h_veps, h_rstd, ahead)
                    if since(g, 0):
                        pool.wait_ge(s_in_psum, now)
                        pool.wait_ge(s_tok_made, now)
                    eng.tensor_tensor(s[0:ROWS, 0:GP], h_c[0:ROWS], wide(st2[0:ROWS, 3, :]),
                                      ALU.mult).then_inc(s_ready, 1)
                if attend:
                    rstd(st3, a_var, a_veps, a_rstd, now)

            turns(pool, turn)

        @block.scalar
        def _(act):
            eng = nc.scalar
            act.dma_start(tokw_raw[:], tok_w).then_inc(tokw_loaded, 16)
            for dst, src in ((tokb_sb, tok_b), (gamma_sb, tok_gamma), (beta_sb, tok_beta), (rb2_sb, router_b2)):
                act.dma_start(dst[:], src.partition_broadcast(128)).then_inc(rows_loaded, 16)
            act.dma_start(e_raw[:].rearrange("i (h j) -> i h j", h=HEADS),
                          attn_e.rearrange("h i j -> i h j")).then_inc(e_loaded, 16)

            def turn(g, project, attend, experts):
                ahead, now, last, before = counts(act, g)

                def qs_copy(i):
                    act.wait_ge(qs_in_psum[i], now)
                    if i == 0 and since(g, 1):
                        act.wait_ge(om_in_psum[GP - 1], last)
                    eng.copy(qs[:, :, i, :], ring[i % 2][:, 0:N].rearrange("p (c t) -> p c t", c=GC)
                             ).then_inc(qs_copied[i], 1)

                def z_copy(i):
                    act.wait_ge(z_in_psum[i], now)
                    if i == 0 and since(g, 1):
                        act.wait_ge(r_in_psum, last)
                    eng.copy(z_t[:, :, i, :].rearrange("p h (s u) -> p s h u", s=2)[:, :, :, 0:T],
                             zb[i % 2][:, 0:2 * HP * T].rearrange("p (s h t) -> p s h t", s=2, h=HP)
                             ).then_inc(z_copied[i], 1)

                def h1_relu(e):
                    act.wait_ge(h1_in_psum[e], last)
                    if since(g, 2):
                        act.wait_ge(h2_in_psum[e], before)
                    eng.activation(h1[:, e, :], ring[e % 2][:, 0:N], ACT.Relu,
                                   bias=b1_sb[:, e:e + 1]).then_inc(h1_made[e], 1)

                def h2_relu(e):
                    act.wait_ge(h2_in_psum[e], last)
                    if since(g, 2):
                        act.wait_ge(h2_weighted[e], before)
                    eng.activation(h2[:, e, :], ring[(e + 1) % 2][:, 0:N], ACT.Relu,
                                   bias=b2_sb[:, e:e + 1]).then_inc(h2_made[e], 1)

                if attend:
                    qs_copy(0)
                if experts:
                    act.wait_ge(rh_in_psum, last)
                    if since(g, 2):
                        act.wait_ge(l_in_psum, before)
                    if not since(g, 2):
                        act.wait_ge(rest_loaded, 15 * 16)
                        act.wait_ge(cleared, 10)
                    eng.activation(rh[:, :, 0:T], tb[0:RHID, 0:N].rearrange("p (c t) -> p c t", c=GC),
                                   ACT.Relu, bias=rb1_sb[:, 0:1]).then_inc(rh_made, 1)
                if attend:
                    qs_copy(2)
                if project:
                    act.wait_ge(x_in_psum, ahead)
                    if since(g, 0):
                        act.wait_ge(y_in_psum, now)
                    eng.copy(x_t[:], pairs_of(tb, BROWS)).then_inc(x_copied, 1)
                if experts:
                    h1_relu(0)
                    h1_relu(1)
                    act.wait_ge(l_centred, last)
                    eng.activation(ex[0:ROWS], logits_c[0:ROWS], ACT.Exp).then_inc(ex_made, 1)
                if project:
                    act.wait_ge(y_centred, ahead)
                    eng.activation(y_sq[0:ROWS], y_c[0:ROWS], ACT.Square, scale=D ** -0.5).then_inc(y_squared, 1)
                if experts:
                    h1_relu(2)
                if attend:
                    z_copy(0)
                    z_copy(1)
                if experts:
                    act.wait_ge(probs_made, last)
                    eng.activation(ex2[0:ROWS], probs[0:ROWS], ACT.Exp).then_inc(ex2_made, 1)
                if attend:
                    z_copy(2)
                    z_copy(3)
                if project:
                    act.wait_ge(h_centred, ahead)
                    eng.activation(h_sq[0:ROWS], h_c[0:ROWS], ACT.Square, scale=D ** -0.5).then_inc(h_squared, 1)
                if experts:
                    act.wait_ge(gt_in_psum, last)
                    if since(g, 2):
                        act.wait_ge(o_in_psum, before)
                    eng.copy(gate_t[:, 0:ROWS + 1], tb[:, 0:ROWS + 1]).then_inc(gt_copied, 1)
                    h2_relu(0)
                if attend:
                    act.wait_ge(a_centred, now)
                    eng.activation(a_sq[0:ROWS], a_c[0:ROWS], ACT.Square, scale=D ** -0.5).then_inc(a_squared, 1)
                if experts:
                    h2_relu(1)
                    h2_relu(2)
                if project:
                    if not since(g, 0):
                        act.wait_ge(cleared, 10)
                    act.wait_ge(s_in_psum, ahead)
                    if since(g, 0):
                        act.wait_ge(qs_in_psum[HP - 1], now)
                        act.wait_ge(om_in_psum[GP - 1], now)
                    eng.copy(s_split[0:64], clips_of(tb)[0:64]).then_inc(s_upper, 1)
                    eng.copy(s_feat[0:64, :, 0:T], clips_of(tb)[0:64]).then_inc(s_feat_top, 1)
                    eng.copy(s_feat[64:128, :, 64:64 + T], clips_of(tb)[0:64]).then_inc(s_feat_made, 1)
                if attend:
                    act.wait_ge(a_in_psum, now)
                    if since(g, 1):
                        act.wait_ge(h1_in_psum[EP - 1], last)
                    eng.copy(h_split[0:64], clips_of(tb)[0:64]).then_inc(a_upper, 1)

            turns(act, turn)

        @block.vector
        def _(dve):
            eng = nc.vector
            eng.memset(xin[:], 0.0).then_inc(xin_cleared, 1)
            dve.wait_ge(w_in_psum, 1)
            eng.tensor_copy(tokw_t[:], yb[:, 0:2 * D].rearrange("p (h i) -> p h i", h=2)).then_inc(w_copied, 1)
            for tile in (s_feat, rh, gate_parts, b3_raw, w2_diag, s, a_n):
                eng.memset(tile[:], 0.0).then_inc(cleared, 1)
            dve.wait_ge(half_mask, 1)
            eng.tensor_copy(causal[64:128, :], causal[0:64, :]).then_inc(mask_made, 1)
            dve.wait_ge(cleared, 10)
            dve.wait_ge(rows_loaded, 64)

            def split_weights():
                dve.wait_ge(e_in_psum, 1)
                eng.tensor_copy(e_t[:], ring[0][:, 0:HP * D].rearrange("p (h i) -> p h i", h=HP)).then_inc(e_copied, 1)
                dve.wait_ge(q_loaded, 6 * 16)
                for k, (raw, hi) in enumerate(((q_raw, q_hi), (w1_raw, w1_hi), (rw1_raw, rw1_hi))):
                    eng.tensor_copy(hi[:], raw[:]).then_inc(q_rounded, 1)
                for k, (raw, hi, lo) in enumerate(((q_raw, q_hi, q_lo), (w1_raw, w1_hi, w1_lo),
                                                   (rw1_raw, rw1_hi, rw1_lo))):
                    dve.wait_ge(q_rounded, k + 1)
                    eng.tensor_tensor(lo[:], raw[:], hi[:].bitcast(F32), ALU.subtract).then_inc(q_split, 1)
                dve.wait_ge(spread_made, 1)
                eng.tensor_copy(spread[:].rearrange("p a e m -> p (a e m)"), spread_raw[:]).then_inc(spread_rounded, 1)
                dve.wait_ge(rest_loaded, 15 * 16)
                eng.tensor_copy(b3_hi[:], b3_raw[:]).then_inc(q_rounded, 1)
                dve.wait_ge(q_rounded, 4)
                eng.tensor_tensor(b3_lo[:], b3_raw[:], b3_hi[:].bitcast(F32), ALU.subtract).then_inc(q_split, 1)

            def row(v, n):
                return v.unsqueeze(1).to_broadcast([ROWS, GP, n])

            def wide(v, n):
                return v.unsqueeze(2).to_broadcast([ROWS, GP, n])

            def sum_rows(out_, in_, done):
                eng.tensor_reduce(out_, in_, axis=AX.X, op=ALU.add).then_inc(done, 1)

            def centre(out_, in_, sums, done):
                eng.scalar_tensor_tensor(out_, wide(sums, D), -1.0 / D, in_, ALU.mult, ALU.add).then_inc(done, 1)

            def turn(g, project, attend, experts):
                ahead, now, last, before = counts(dve, g)

                def h_of(k):
                    return hbuf[0:ROWS, bass.ds(k, 1), :, :].rearrange("p g a d -> p (g a) d")

                def mask(i):
                    dve.wait_ge(om_in_psum[i], now)
                    if since(g, 1):
                        dve.wait_ge(z_in_psum[i], last)
                    eng.tensor_tensor(omega[0:ROWS, 2 * i:2 * i + 2, :, :].rearrange("p c h t -> p (c h t)"),
                                      om[i % 2][0:ROWS, 0:N], causal[0:ROWS, :], ALU.mult).then_inc(om_masked[i], 1)

                def weigh(e):
                    dve.wait_ge(h2_made[e], last)
                    dve.wait_ge(gate_in_psum[e], last)
                    if e == 0 and since(g, 2):
                        dve.wait_ge(o_in_psum, before)
                    eng.tensor_tensor(h2w[:, e, :, 0:T], clips_of(zb[e % 2]),
                                      h2[:, e, :].rearrange("p (c t) -> p c t", c=GC),
                                      ALU.mult).then_inc(h2_weighted[e], 1)

                if attend:
                    for i in (1, 3):
                        dve.wait_ge(qs_in_psum[i], now)
                        if i == 1 and since(g, 1):
                            dve.wait_ge(om_in_psum[GP - 1], last)
                        eng.tensor_copy(qs[:, :, i, :], ring[i % 2][:, 0:N].rearrange("p (c t) -> p c t", c=GC)
                                        ).then_inc(qs_copied[i], 1)
                if experts:
                    dve.wait_ge(l_in_psum, last)
                    eng.tensor_tensor(logits[0:ROWS], l_ps[0:ROWS], row(rb2_sb[0:ROWS, :], EXPERTS),
                                      ALU.add).then_inc(l_added, 1)
                if project:
                    dve.wait_ge(y_in_psum, ahead)
                    eng.tensor_tensor(y[0:ROWS], y_ps[0:ROWS], row(tokb_sb[0:ROWS, :], D),
                                      ALU.add).then_inc(y_added, 1)
                if experts:
                    dve.wait_ge(l_added, last)
                    eng.tensor_reduce(rst[0:ROWS, 0, :], logits[0:ROWS], axis=AX.X, op=ALU.max).then_inc(l_max, 1)
                if project:
                    dve.wait_ge(y_added, ahead)
                    sum_rows(st1[0:ROWS, 0, :], y[0:ROWS], y_summed)
                if experts:
                    dve.wait_ge(l_max, last)
                    eng.tensor_tensor(logits_c[0:ROWS], logits[0:ROWS], wide(rst[0:ROWS, 0, :], EXPERTS),
                                      ALU.subtract).then_inc(l_centred, 1)
                if project:
                    dve.wait_ge(y_summed, ahead)
                    centre(y_c[0:ROWS], y[0:ROWS], st1[0:ROWS, 0, :], y_centred)
                if project:
                    dve.wait_ge(y_squared, ahead)
                    sum_rows(st1[0:ROWS, 1, :], y_sq[0:ROWS], y_var)
                    if not since(g, 0):
                        split_weights()
                if attend:
                    mask(0)
                if experts:
                    dve.wait_ge(ex_made, last)
                    sum_rows(rst[0:ROWS, 1, :], ex[0:ROWS], ex_summed)
                if attend:
                    mask(1)
                if experts:
                    dve.wait_ge(ex_summed, last)
                    eng.reciprocal(rst[0:ROWS, 2, :], rst[0:ROWS, 1, :]).then_inc(ex_inv, 1)
                    dve.wait_ge(ex_inv, last)
                    eng.tensor_tensor(probs[0:ROWS], ex[0:ROWS], wide(rst[0:ROWS, 2, :], EXPERTS),
                                      ALU.mult).then_inc(probs_made, 1)
                if attend:
                    mask(2)
                if experts:
                    shape = [ROWS, GP, EXPERTS, EXPERTS]
                    other = probs[0:ROWS].unsqueeze(2).to_broadcast(shape)
                    own = probs[0:ROWS].unsqueeze(3).to_broadcast(shape)
                    dve.wait_ge(probs_made, last)
                    eng.tensor_tensor(above[0:ROWS], other, own, ALU.is_gt).then_inc(above_made, 1)
                    eng.tensor_tensor(tied[0:ROWS], other, own, ALU.is_ge).then_inc(tied_made, 1)
                if attend:
                    mask(3)
                if experts:
                    dve.wait_ge(tied_made, last)
                    eng.tensor_tensor(tied_e[0:ROWS], tied[0:ROWS],
                                      earlier[0:ROWS].unsqueeze(1).to_broadcast(shape), ALU.mult).then_inc(tied_cut, 1)
                    dve.wait_ge(above_made, last)
                    dve.wait_ge(tied_cut, last)
                    eng.tensor_tensor(beats[0:ROWS], above[0:ROWS], tied_e[0:ROWS], ALU.max).then_inc(beats_made, 1)
                    dve.wait_ge(beats_made, last)
                    eng.tensor_reduce(rank[0:ROWS], beats[0:ROWS], axis=AX.X, op=ALU.add).then_inc(rank_made, 1)
                    dve.wait_ge(rank_made, last)
                    dve.wait_ge(ex2_made, last)
                    eng.scalar_tensor_tensor(picked[0:ROWS], rank[0:ROWS], 1.5, ex2[0:ROWS], ALU.is_lt,
                                             ALU.mult).then_inc(picked_made, 1)
                    dve.wait_ge(picked_made, last)
                    sum_rows(rst[0:ROWS, 3, :], picked[0:ROWS], picked_sum)
                if project:
                    dve.wait_ge(h_ready, ahead)
                    sum_rows(st2[0:ROWS, 0, :], h[0:ROWS], h_summed)
                if experts:
                    dve.wait_ge(picked_sum, last)
                    eng.reciprocal(rst[0:ROWS, 4, :], rst[0:ROWS, 3, :]).then_inc(picked_inv, 1)
                if project:
                    dve.wait_ge(h_summed, ahead)
                    centre(h_c[0:ROWS], h[0:ROWS], st2[0:ROWS, 0, :], h_centred)
                    eng.tensor_copy(h_of(g + 1), h[0:ROWS]).then_inc(h_kept, 1)
                if experts:
                    dve.wait_ge(picked_inv, last)
                    eng.tensor_tensor(gate[0:ROWS], picked[0:ROWS], wide(rst[0:ROWS, 4, :], EXPERTS),
                                      ALU.mult).then_inc(gate_made, 1)
                    dve.wait_ge(gate_made, last)
                    if since(g, 2):
                        dve.wait_ge(gt_in_psum, before)
                    eng.tensor_copy(gate_up[0:ROWS].bitcast(F32R), gate[0:ROWS]).then_inc(gate_upper, 1)
                    dve.wait_ge(gate_upper, last)
                    eng.tensor_tensor(gate_low[0:ROWS], gate[0:ROWS], gate_up[0:ROWS], ALU.subtract).then_inc(gate_split, 1)
                if project:
                    dve.wait_ge(h_squared, ahead)
                    sum_rows(st2[0:ROWS, 1, :], h_sq[0:ROWS], h_var)
                if attend:
                    dve.wait_ge(r_in_psum, now)
                    dve.wait_ge(h_kept, now)
                    eng.tensor_tensor(a[0:ROWS], y_ps[0:ROWS], h_of(g), ALU.add).then_inc(a_ready, 1)
                    dve.wait_ge(a_ready, now)
                    sum_rows(st3[0:ROWS, 0, :], a[0:ROWS], a_summed)
                if attend:
                    dve.wait_ge(a_summed, now)
                    centre(a_c[0:ROWS], a[0:ROWS], st3[0:ROWS, 0, :], a_centred)
                    eng.tensor_copy(h_of(g), a[0:ROWS]).then_inc(a_kept, 1)
                if experts:
                    weigh(0)
                if attend:
                    dve.wait_ge(a_squared, now)
                    sum_rows(st3[0:ROWS, 1, :], a_sq[0:ROWS], a_var)
                if experts:
                    weigh(1)
                if attend:
                    dve.wait_ge(a_rstd, now)
                    if since(g, 1):
                        dve.wait_ge(a_in_psum, last)
                    eng.tensor_tensor(a_n[0:ROWS, 0:GP], a_c[0:ROWS], wide(st3[0:ROWS, 3, :], D),
                                      ALU.mult).then_inc(a_normed, 1)
                if experts:
                    weigh(2)
                if project:
                    dve.wait_ge(s_ready, ahead)
                    if since(g, 0):
                        dve.wait_ge(z_in_psum[GP - 1], now)
                    for side in range(2):
                        for par in range(2):
                            last_copy = eng.tensor_copy(
                                s_tok[64 * par:64 * par + T, :, 64 * par:64 * par + D].rearrange(
                                    "p (a c) d -> p a c d", c=2)[:, :, side, :],
                                s[64 * side:64 * side + T, 0:GP, :])
                    last_copy.then_inc(s_tok_made, 1)
                    dve.wait_ge(s_feat_made, ahead)
                    dve.wait_ge(s_upper, ahead)
                    eng.tensor_tensor(s_split[64:128], clips_of(tb)[0:64], s_split[0:64].bitcast(F32),
                                      ALU.subtract).then_inc(s_split_made, 1)
                if attend:
                    dve.wait_ge(a_upper, now)
                    eng.tensor_tensor(h_split[64:128], clips_of(tb)[0:64], h_split[0:64].bitcast(F32),
                                      ALU.subtract).then_inc(a_split_made, 1)
                if experts:
                    dve.wait_ge(o_in_psum, last)
                    dve.wait_ge(a_kept, last)
                    eng.tensor_tensor(h_of(g - 1), y_ps[0:ROWS], h_of(g - 1), ALU.add).then_inc(o_added, 1)

            turns(dve, turn)

        @block.tensor
        def _(pe):
            mm, tr = nc.tensor.matmul, nc.tensor.transpose
            pe.wait_ge(consts, 1)
            pe.wait_ge(tokw_loaded, 16)
            for half in range(2):
                done = tr(yb[0:128, D * half:D * (half + 1)], tokw_raw[:, BLK * half:BLK * (half + 1)],
                          ident[0:D, 0:D])
            done.then_inc(w_in_psum, 1)

            def split_matmul(out_, hi, lo, moving):
                mm(out_, hi, moving, start=True, stop=False)
                return mm(out_, lo, moving, start=False, stop=True)

            def turn(g, project, attend, experts):
                ahead, now, last, before = counts(pe, g)

                def qs_product(i):
                    if i == 0:
                        pe.wait_ge(s_split_made, now)
                        if since(g, 1):
                            pe.wait_ge(h2_made[EP - 1], before)
                    if i >= 2:
                        pe.wait_ge(qs_copied[i - 2], now)
                    split_matmul(ring[i % 2][:, 0:N], q_hi[:, i, :], q_lo[:, i, :],
                                 s_split[:].rearrange("p c t -> p (c t)")).then_inc(qs_in_psum[i], 1)

                def omega_product(i):
                    if i == 0:
                        pe.wait_ge(qs_copied[HP - 2], now)
                        pe.wait_ge(qs_copied[HP - 1], now)
                        pe.wait_ge(s_feat_made, now)
                    if i >= 2:
                        pe.wait_ge(om_masked[i - 2], now)
                    elif since(g, 1):
                        pe.wait_ge(om_masked[i + 2], last)
                    for c in range(2):
                        done = mm(om[i % 2][0:ROWS, HP * T * c:HP * T * (c + 1)], s_feat[:, 2 * i + c, 0:ROWS],
                                  qs[:, 2 * i + c, :, :].rearrange("p h t -> p (h t)"), start=True, stop=True)
                    done.then_inc(om_in_psum[i], 1)

                def z_product(i):
                    pe.wait_ge(om_masked[i], now)
                    if i == 0:
                        pe.wait_ge(s_tok_made, now)
                        if since(g, 2):
                            pe.wait_ge(h2_weighted[2], before)
                    elif i == 1 and since(g, 2):
                        pe.wait_ge(h2_weighted[1], before)
                    elif i >= 2:
                        pe.wait_ge(z_copied[i - 2], now)
                    for c in range(2):
                        done = mm(zb[i % 2][:, HP * T * c:HP * T * (c + 1)], s_tok[0:ROWS, 2 * i + c, :],
                                  omega[0:ROWS, 2 * i + c, :, :].rearrange("p h t -> p (h t)"), start=True, stop=True)
                    done.then_inc(z_in_psum[i], 1)

                def gate_spread(e):
                    if e == 0:
                        pe.wait_ge(gt_copied, last)
                    if e == 2:
                        pe.wait_ge(h2_weighted[0], last)
                    elif attend:
                        pe.wait_ge(z_copied[2 + e], now)
                    else:
                        pe.wait_ge(h2_weighted[2 - e], before)
                    for p in range(GP):
                        done = mm(zb[e % 2][:, 128 * p:128 * p + ROWS + 1], spread[:, p, e, :], gate_t[:, 0:ROWS + 1],
                                  start=True, stop=True)
                    done.then_inc(gate_in_psum[e], 1)

                def h1_product(e):
                    if e == 2:
                        pe.wait_ge(h1_made[0], last)
                    elif attend:
                        pe.wait_ge(qs_copied[2 + e], now)
                    elif e == 0:
                        pe.wait_ge(h2_made[EP - 1], before)
                    split_matmul(ring[e % 2][:, 0:N], w1_hi[:, e, :], w1_lo[:, e, :],
                                 h_split[:].rearrange("p c t -> p (c t)")).then_inc(h1_in_psum[e], 1)

                def head_sum(p):
                    pe.wait_ge(z_copied[p], now)
                    if p == 0 and project:
                        pe.wait_ge(y_added, ahead)
                    elif p == 0 and experts:
                        pe.wait_ge(l_added, last)
                    for i in range(HP):
                        done = mm(yb[0:ROWS, D * p:D * (p + 1)], z_t[:, i, p, 0:ROWS], e_t[:, i, :],
                                  start=i == 0, stop=i == HP - 1)
                    return done

                def last_layer(e):
                    pe.wait_ge(h2_weighted[e], last)
                    for p in range(GP):
                        done = mm(yb[0:ROWS, D * p:D * (p + 1)],
                                  h2w[:, e, 2 * p:2 * p + 2, :].rearrange("p c u -> p (c u)")[:, 0:ROWS],
                                  w3_sb[:, e, :], start=e == 0 and p == 0, stop=e == EP - 1,
                                  skip_group_check=True)
                    return done

                def h2_product(e):
                    pe.wait_ge(h1_made[e], last)
                    if e < 2:
                        pe.wait_ge(h1_made[e + 1], last)
                    else:
                        pe.wait_ge(h2_made[0], last)
                    mm(ring[(e + 1) % 2][:, 0:N], w2_diag[:, e, :], h1[:, e, :], start=True,
                       stop=True).then_inc(h2_in_psum[e], 1)

                if attend:
                    if not since(g, 1):
                        pe.wait_ge(e_copied, 1)
                        pe.wait_ge(q_split, 4)
                        pe.wait_ge(spread_rounded, 1)
                    qs_product(0)
                    qs_product(1)
                if experts:
                    pe.wait_ge(a_split_made, last)
                    split_matmul(tb[0:RHID, 0:N], rw1_hi[:], rw1_lo[:],
                                 h_split[:].rearrange("p c t -> p (c t)")).then_inc(rh_in_psum, 1)
                if attend:
                    qs_product(2)
                    qs_product(3)
                if project:
                    pe.wait_ge(x_loaded, 32 * ahead)
                    if experts:
                        pe.wait_ge(rh_made, last)
                    elif attend:
                        pe.wait_ge(s_split_made, now)
                    for p in range(GP):
                        done = tr(tb[:, 128 * p:128 * p + BROWS], xin[0:BROWS, p, :], ident[0:BROWS, 0:BROWS])
                    done.then_inc(x_in_psum, 1)
                if experts:
                    h1_product(0)
                    h1_product(1)
                    pe.wait_ge(rh_made, last)
                    if since(g, 2):
                        pe.wait_ge(o_added, before)
                    for p in range(GP):
                        done = mm(yb[0:ROWS, EXPERTS * p:EXPERTS * (p + 1)],
                                  rh[:, 2 * p:2 * p + 2, :].rearrange("p c u -> p (c u)")[:, 0:ROWS], rw2_sb[:],
                                  start=True, stop=True)
                    done.then_inc(l_in_psum, 1)
                if project:
                    pe.wait_ge(w_copied, 1)
                    pe.wait_ge(x_copied, ahead)
                    if experts:
                        pe.wait_ge(l_added, last)
                    for p in range(GP):
                        for half in range(2):
                            done = mm(yb[0:ROWS, D * p:D * (p + 1)], x_t[:, p, half:half + ROWS],
                                      tokw_t[:, half, :], start=half == 0, stop=half == 1)
                    done.then_inc(y_in_psum, 1)
                if not since(g, 0):
                    pe.wait_ge(e_loaded, 16)
                    for i in range(HP):
                        done = tr(ring[0][:, D * i:D * (i + 1)], e_raw[:, 128 * i:128 * (i + 1)], ident[0:D, 0:D])
                    done.then_inc(e_in_psum, 1)
                if attend:
                    omega_product(0)
                    omega_product(1)
                if experts:
                    h1_product(2)
                if attend:
                    z_product(0)
                    omega_product(2)
                    z_product(1)
                    omega_product(3)
                    z_product(2)
                    head_sum(0)
                    z_product(3)
                    head_sum(1)
                    head_sum(2)
                    head_sum(3).then_inc(r_in_psum, 1)
                if experts:
                    pe.wait_ge(gate_split, last)
                    if project:
                        pe.wait_ge(x_copied, ahead)
                    else:
                        pe.wait_ge(rh_made, last)
                    tr(tb[:, 0:ROWS + 1], gate_parts[0:ROWS + 1, :], ident[0:ROWS + 1, 0:ROWS + 1]
                       ).then_inc(gt_in_psum, 1)
                    h2_product(0)
                    gate_spread(0)
                    h2_product(1)
                    gate_spread(1)
                    h2_product(2)
                    gate_spread(2)
                if project:
                    pe.wait_ge(s_ready, ahead)
                    if experts:
                        pe.wait_ge(gt_copied, last)
                    else:
                        pe.wait_ge(x_copied, ahead)
                    for p in range(GP):
                        done = tr(tb[:, 128 * p:128 * p + ROWS], s[0:ROWS, p:p + 2, :].rearrange("p a d -> p (a d)"), ident[0:ROWS, 0:ROWS])
                    done.then_inc(s_in_psum, 1)
                if experts:
                    if attend:
                        pe.wait_ge(a_ready, now)
                    else:
                        pe.wait_ge(l_added, last)
                    last_layer(0)
                    last_layer(1)
                    for p in range(GP):
                        for part in (b3_hi, b3_lo):
                            mm(yb[0:ROWS, D * p:D * (p + 1)], gate_t[:, 0:ROWS], part[:, p, :], start=False,
                               stop=False, skip_group_check=True)
                if attend:
                    pe.wait_ge(a_normed, now)
                    if project:
                        pe.wait_ge(s_split_made, ahead)
                    elif experts:
                        pe.wait_ge(gt_copied, last)
                    for p in range(GP):
                        done = tr(tb[:, 128 * p:128 * p + ROWS], a_n[0:ROWS, p:p + 2, :].rearrange("p a d -> p (a d)"), ident[0:ROWS, 0:ROWS])
                    done.then_inc(a_in_psum, 1)
                if experts:
                    last_layer(2).then_inc(o_in_psum, 1)

            turns(pe, turn)


_INS = ['x', 'L0_tok_W', 'L0_tok_b', 'L0_tok_gamma', 'L0_tok_beta', 'L0_attn_Q', 'L0_attn_E',
        'L0_ffn_router_w1', 'L0_ffn_router_b1', 'L0_ffn_router_w2', 'L0_ffn_router_b2',
        'L0_ffn_expert_w1', 'L0_ffn_expert_b1', 'L0_ffn_expert_w2', 'L0_ffn_expert_b2',
        'L0_ffn_expert_w3', 'L0_ffn_expert_b3']
_OUTS = [((64, 45, 64), 'float32')]


def kernel(**inputs):
    import numpy as _np
    import concourse.bacc as _bacc
    from concourse import mybir as _mybir
    from concourse.bass_utils import run_bass_kernel_spmd as _run

    nc = _bacc.Bacc("TRN2", target_bir_lowering=False, num_devices=1)
    arrays, args = {}, []
    for name in _INS:
        a = _np.ascontiguousarray(inputs[name])
        arrays[f"in_{name}_dram"] = a
        args.append(nc.dram_tensor(f"in_{name}_dram", a.shape, _mybir.dt.from_np(a.dtype), kind="ExternalInput").ap())
    for i, (shape, dtype) in enumerate(_OUTS):
        dt = _mybir.dt.from_np(_np.dtype(dtype))
        args.append(nc.dram_tensor(f"out_{i}_dram", shape, dt, kind="ExternalOutput").ap())
    audio_tower(nc, *args)
    r = _run(nc, [arrays], core_ids=[0])
    got = tuple(r.results[0][f"out_{i}_dram"] for i in range(len(_OUTS)))
    return got[0]
```

```python
import concourse.bass as bass
from concourse import mybir
from contextlib import ExitStack



def audio_tower(nc, x, tok_w, tok_b, tok_gamma, tok_beta, attn_q, attn_e, router_w1, router_b1,
                router_w2, router_b2, w1, b1, w2, b2, w3, b3, out):
    F32, F32R = mybir.dt.float32, mybir.dt.float32r
    ALU, ACT, AX = mybir.AluOpType, mybir.ActivationFunctionType, mybir.AxisListType

    CLIPS, STEPS, FREQ = x.shape
    D, PATCH_IN = tok_w.shape
    HEADS = attn_q.shape[0]
    EXPERTS, _, HID = w1.shape
    RHID = router_w1.shape[1]
    T = out.shape[1]
    EPS = 1e-5
    BLK = PATCH_IN // 2
    NBLK = T + 1
    GC = 8
    GP = GC // 2
    G = CLIPS // GC
    N = GC * T
    ROWS = 64 + T
    BROWS = 64 + NBLK
    HP = HEADS // 2
    EP = EXPERTS // 2
    XCOLS = NBLK * BLK

    x_blocks = x.rearrange("b r f -> b (r f)")[:, 0:XCOLS].rearrange(
        "(p side) (k c) -> side k p c", side=2, c=BLK)
    out_rows = out.rearrange("(p side) t d -> side t p d", side=2)

    with ExitStack() as ctx:
        def sb(name, shape, dt=F32):
            return ctx.enter_context(nc.sbuf_tensor(name, shape, dt))

        def pb(name):
            return ctx.enter_context(nc.psum_tensor(name, [128, 512], F32))

        def sem(name):
            return ctx.enter_context(nc.semaphore(name))

        ident = sb("ident", [128, 128])
        causal = sb("causal", [128, N])
        earlier = sb("earlier", [128, EXPERTS, EXPERTS])
        minus_half = sb("minus_half", [128, GP])
        q_raw = sb("q_raw", [128, HP, 128])
        q_hi = sb("q_hi", [128, HP, 128], F32R)
        q_lo = sb("q_lo", [128, HP, 128], F32R)
        w1_raw = sb("w1_raw", [128, EP, 128])
        w1_hi = sb("w1_hi", [128, EP, 128], F32R)
        w1_lo = sb("w1_lo", [128, EP, 128], F32R)
        rw1_raw = sb("rw1_raw", [128, RHID])
        rw1_hi = sb("rw1_hi", [128, RHID], F32R)
        rw1_lo = sb("rw1_lo", [128, RHID], F32R)
        e_raw = sb("e_raw", [D, HEADS * D])
        tokw_raw = sb("tokw_raw", [D, PATCH_IN])
        e_t = sb("e_t", [128, HP, D + 1])
        tokw_whole = sb("tokw_whole", [128, 2, D])
        tokw_t = sb("tokw_t", [128, 2, D])
        tokb_c = sb("tokb_c", [128, D])
        w_sums = sb("w_sums", [128, 3])
        w2_diag = sb("w2_diag", [128, EP, 128])
        w3_sb = sb("w3_sb", [128, EP, D])
        rw2_sb = sb("rw2_sb", [RHID, EXPERTS])
        b1_sb = sb("b1_sb", [128, EP])
        b2_sb = sb("b2_sb", [128, EP])
        rb1_sb = sb("rb1_sb", [RHID, 1])
        b3_raw = sb("b3_raw", [128, GP, D])
        b3_hi = sb("b3_hi", [128, GP, D], F32R)
        b3_lo = sb("b3_lo", [128, GP, D], F32R)
        spread_raw = sb("spread_raw", [128, GP * EP * 128])
        spread = sb("spread", [128, GP, EP, 128], F32R)
        tokb_sb = sb("tokb_sb", [128, D])
        gamma_sb = sb("gamma_sb", [128, D])
        beta_sb = sb("beta_sb", [128, D])
        rb2_sb = sb("rb2_sb", [128, EXPERTS])

        xin = sb("xin", [128, GP, BLK])
        x_t = sb("x_t", [128, GP, BROWS])
        y_c = sb("y_c", [128, GP, D])
        y_sq = sb("y_sq", [128, GP, D + 1])
        y_g = sb("y_g", [128, GP, D])
        y_n = sb("y_n", [128, GP, D])
        hbuf = sb("hbuf", [128, G, GP, D + 1])
        h_c = sb("h_c", [128, GP, D])
        h_sq = sb("h_sq", [128, GP, D + 1])
        h = sb("h", [128, GP, D + 1])
        s = sb("s", [128, GP + 1, D])
        st1 = sb("st1", [128, 2, GP])
        st2 = sb("st2", [128, 2, GP])
        st3 = sb("st3", [128, 2, GP])

        s_split = sb("s_split", [128, GC, T], F32R)
        s_feat = sb("s_feat", [128, GC, 128])
        s_tok = sb("s_tok", [128, GC, 128])
        qs = sb("qs", [128, GC, HP, T])
        omega = sb("omega", [128, GC, HP, T])
        z_t = sb("z_t", [128, HP, GP, 128])
        a_c = sb("a_c", [128, GP, D])
        a_sq = sb("a_sq", [128, GP, D + 1])
        a = sb("a", [128, GP, D + 1])
        a_n = sb("a_n", [128, GP + 1, D])

        h_split = sb("h_split", [128, GC, T], F32R)
        rh = sb("rh", [RHID, GC, 64])
        logits = sb("logits", [128, GP, EXPERTS])
        logits_c = sb("logits_c", [128, GP, EXPERTS])
        ex = sb("ex", [128, GP, EXPERTS])
        probs = sb("probs", [128, GP, EXPERTS])
        ex2 = sb("ex2", [128, GP, EXPERTS])
        picked = sb("picked", [128, GP, EXPERTS])
        rank = sb("rank", [128, GP, EXPERTS])
        above = sb("above", [128, GP, EXPERTS, EXPERTS])
        tied = sb("tied", [128, GP, EXPERTS, EXPERTS])
        tied_e = sb("tied_e", [128, GP, EXPERTS, EXPERTS])
        beats = sb("beats", [128, GP, EXPERTS, EXPERTS])
        rst = sb("rst", [128, 5, GP])
        gate = sb("gate", [128, GP, EXPERTS])
        gate_parts = sb("gate_parts", [128, 128])
        gate_t = sb("gate_t", [128, 128], F32R)
        h1 = sb("h1", [128, EP, N])
        h2 = sb("h2", [128, EP, N])
        h2w = sb("h2w", [128, EP, GC, 64])
        GATES = GP * EXPERTS
        gate_up = gate_parts[:, 0:GATES].rearrange("p (a e) -> p a e", a=GP)
        gate_low = gate_parts[:, GATES:2 * GATES].rearrange("p (a e) -> p a e", a=GP)

        ring = [pb("ring0"), pb("ring1")]
        om = [pb("om0"), pb("om1")]
        zb = [pb("zb0"), pb("zb1")]
        tb = pb("tb")
        yb = pb("yb")

        def pairs_of(bank, width):
            return bank[:, :].rearrange("p (a c) -> p a c", a=GP)[:, :, 0:width]

        def clips_of(bank):
            return bank[:, :].rearrange("p (c u) -> p c u", u=64)[:, :, 0:T]

        y_ps = yb[:, 0:GP * D].rearrange("p (a d) -> p a d", a=GP)
        r_ps = yb[:, 0:GP * (D + 1)].rearrange("p (a d) -> p a d", a=GP)
        l_ps = yb[:, 0:GP * EXPERTS].rearrange("p (a e) -> p a e", a=GP)

        x_loaded, stored = sem("x_loaded"), sem("stored")
        tokw_loaded, q_loaded, e_loaded, rows_loaded, rest_loaded = (
            sem(n) for n in ("tokw_loaded", "q_loaded", "e_loaded", "rows_loaded", "rest_loaded"))
        xin_cleared, cleared, consts = sem("xin_cleared"), sem("cleared"), sem("consts")
        half_mask, mask_made = sem("half_mask"), sem("mask_made")
        pool_step = sem("pool_step")
        e_in_psum, e_copied = sem("e_in_psum"), sem("e_copied")
        w_in_psum, w_copied, w_summed, w_centred, q_rounded, q_split = (
            sem(n) for n in ("w_in_psum", "w_copied", "w_summed", "w_centred", "q_rounded", "q_split"))
        x_in_psum, x_copied, y_in_psum = sem("x_in_psum"), sem("x_copied"), sem("y_in_psum")
        y_added, y_squared, y_var = sem("y_added"), sem("y_squared"), sem("y_var")
        y_scaled, y_rstd, y_normed, h_ready = (sem(n) for n in ("y_scaled", "y_rstd", "y_normed", "h_ready"))
        h_summed, h_centred, h_squared, h_var, h_rstd, s_ready = (
            sem(n) for n in ("h_summed", "h_centred", "h_squared", "h_var", "h_rstd", "s_ready"))
        s_in_psum, s_upper, s_feat_top, s_feat_made, s_split_made, s_tok_made = (
            sem(n) for n in ("s_in_psum", "s_upper", "s_feat_top", "s_feat_made", "s_split_made", "s_tok_made"))
        qs_in_psum = [sem(f"qs_in_psum{i}") for i in range(HP)]
        qs_copied = [sem(f"qs_copied{i}") for i in range(HP)]
        om_in_psum = [sem(f"om_in_psum{i}") for i in range(GP)]
        om_masked = [sem(f"om_masked{i}") for i in range(GP)]
        z_in_psum = [sem(f"z_in_psum{i}") for i in range(GP)]
        z_copied = [sem(f"z_copied{i}") for i in range(GP)]
        r_in_psum, a_ready, a_centred, a_squared, a_var, a_rstd, a_normed = (
            sem(n) for n in ("r_in_psum", "a_ready", "a_centred", "a_squared", "a_var", "a_rstd", "a_normed"))
        h_kept, a_kept = sem("h_kept"), sem("a_kept")
        a_in_psum, a_upper, a_split_made = sem("a_in_psum"), sem("a_upper"), sem("a_split_made")
        rh_in_psum, rh_made, l_in_psum, l_added, l_max, l_centred, ex_made = (
            sem(n) for n in ("rh_in_psum", "rh_made", "l_in_psum", "l_added", "l_max", "l_centred", "ex_made"))
        ex_summed, ex_inv, probs_made, ex2_made, above_made, tied_made, tied_cut, beats_made = (
            sem(n) for n in ("ex_summed", "ex_inv", "probs_made", "ex2_made", "above_made", "tied_made",
                             "tied_cut", "beats_made"))
        rank_made, picked_made, picked_sum, picked_inv, gate_made, gate_upper, gate_split = (
            sem(n) for n in ("rank_made", "picked_made", "picked_sum", "picked_inv", "gate_made",
                             "gate_upper", "gate_split"))
        spread_made, spread_rounded = sem("spread_made"), sem("spread_rounded")
        h1_in_psum = [sem(f"h1_in_psum{i}") for i in range(EP)]
        h1_made = [sem(f"h1_made{i}") for i in range(EP)]
        gate_in_psum = [sem(f"gate_in_psum{i}") for i in range(EP)]
        h2_in_psum = [sem(f"h2_in_psum{i}") for i in range(EP)]
        h2_made = [sem(f"h2_made{i}") for i in range(EP)]
        h2_weighted = [sem(f"h2_weighted{i}") for i in range(EP)]
        gt_in_psum, gt_copied, o_in_psum, o_added = (
            sem(n) for n in ("gt_in_psum", "gt_copied", "o_in_psum", "o_added"))

        block = ctx.enter_context(nc.Block())

        def counts(engine, g):
            if isinstance(g, int):
                return g + 2, g + 1, g, g - 1
            return engine.snap(g + 2), engine.snap(g + 1), g, engine.snap(g - 1)

        def turns(engine, turn):
            turn(-1, project=True, attend=False, experts=False)
            turn(0, project=True, attend=True, experts=False)
            turn(1, project=True, attend=True, experts=True)
            with engine.Fori(2, G - 2) as g:
                turn(g, project=True, attend=True, experts=True)
            turn(G - 2, project=True, attend=True, experts=True)
            turn(G - 1, project=False, attend=True, experts=True)
            turn(G, project=False, attend=False, experts=True)

        def since(g, first):
            return not isinstance(g, int) or g >= first

        @block.sync
        def _(sp):
            sp.wait_ge(xin_cleared, 1)

            def load_blocks(group):
                for side in range(2):
                    sp.dma_start(xin[64 * side:64 * side + NBLK, :, :],
                                 x_blocks[side][:, bass.ds(group * GP, GP), :]).then_inc(x_loaded, 16)

            load_blocks(0)
            for half in range(2):
                sp.dma_start(q_raw[64 * half:64 * half + D, :, :].rearrange("i p (s j) -> i (p s) j", s=2),
                             attn_q.rearrange("h i j -> i h j")).then_inc(q_loaded, 16)
            for half in range(2):
                rows = slice(64 * half, 64 * half + D)
                sp.dma_start(rw1_raw[rows, :], router_w1).then_inc(q_loaded, 16)
                sp.dma_start(w1_raw[rows, :, :].rearrange("d p (s h) -> d (p s) h", s=2),
                             w1.rearrange("e d h -> d e h")).then_inc(q_loaded, 16)
            sp.dma_start(rb1_sb[:], router_b1.unsqueeze(1)).then_inc(rest_loaded, 16)
            sp.dma_start(rw2_sb[:], router_w2).then_inc(rest_loaded, 16)
            sp.dma_start(b1_sb[:], b1.rearrange("(p s) h -> (s h) p", s=2),
                         allow_slow_non_contiguous=True).then_inc(rest_loaded, 16)
            sp.dma_start(b2_sb[:], b2.rearrange("(p s) h -> (s h) p", s=2),
                         allow_slow_non_contiguous=True).then_inc(rest_loaded, 16)
            sp.dma_start(w3_sb[:], w3.rearrange("(p s) f o -> (s f) p o", s=2)).then_inc(rest_loaded, 16)
            sp.wait_ge(cleared, 13)
            for half in range(2):
                rows = slice(64 * half, 64 * half + HID)
                sp.dma_start(w2_diag[rows, :, rows],
                             w2.rearrange("(p s) h f -> s h p f", s=2)[half]).then_inc(rest_loaded, 16)
            for p in range(GP):
                for top in (EXPERTS * p, EXPERTS * (GP + p)):
                    sp.dma_start(b3_raw[top:top + EXPERTS, p, :], b3).then_inc(rest_loaded, 16)

            def turn(g, project, attend, experts):
                ahead, now, last, before = counts(sp, g)
                if project and not (isinstance(g, int) and g == G - 2):
                    sp.wait_ge(x_in_psum, ahead)
                    load_blocks(g + 2)
                if experts:
                    sp.wait_ge(o_added, last)
                    for side in range(2):
                        sp.dma_start(out_rows[side][:, bass.ds(g * GP - GP, GP), :],
                                     hbuf[64 * side:64 * side + T, bass.ds(g - 1, 1), :, 0:D].rearrange(
                                         "p g a d -> p (g a) d")).then_inc(stored, 16)

            turns(sp, turn)
            sp.wait_ge(stored, 32 * G)

        @block.gpsimd
        def _(pool):
            eng = nc.gpsimd
            eng.memset(ident[:], 0.0).then_inc(pool_step, 1)
            pool.wait_ge(pool_step, 1)
            eng.affine_select(out=ident[:], in_=ident[:], compare_op=ALU.not_equal, fill=1.0, base=0,
                              pattern=[[-1, 128]], channel_multiplier=1).then_inc(consts, 1)
            eng.memset(minus_half[:], -0.5).then_inc(pool_step, 1)
            eng.memset(earlier[:], 1.0).then_inc(pool_step, 1)
            eng.memset(causal[:], 1.0).then_inc(pool_step, 1)
            pool.wait_ge(pool_step, 4)
            eng.affine_select(out=causal[0:64, :].rearrange("p (c t) -> p c t", c=GC),
                              in_=causal[0:64, :].rearrange("p (c t) -> p c t", c=GC),
                              compare_op=ALU.is_ge, fill=0.0, base=0, pattern=[[0, GC], [1, T]],
                              channel_multiplier=-1).then_inc(half_mask, 1)
            eng.affine_select(out=earlier[:], in_=earlier[:], compare_op=ALU.is_gt, fill=0.0, base=0,
                              pattern=[[1, EXPERTS], [-1, EXPERTS]], channel_multiplier=0).then_inc(consts, 1)
            eng.memset(spread_raw[:], 0.0).then_inc(pool_step, 1)
            for part in range(2):
                pool.wait_ge(pool_step, 5 + part)
                done = eng.affine_select(out=spread_raw[:], in_=spread_raw[:], compare_op=ALU.not_equal, fill=1.0,
                                         base=-GATES * part,
                                         pattern=[[-EXPERTS, GP], [-2, EP], [-1, 2], [0, HID]], channel_multiplier=1)
                done.then_inc(pool_step if part == 0 else spread_made, 1)
            eng.memset(s_tok[:], 0.0).then_inc(cleared, 1)
            eng.memset(z_t[:], 0.0).then_inc(cleared, 1)
            eng.memset(h2w[:], 0.0).then_inc(cleared, 1)

            def rstd(st, var, rstd_, value):
                pool.wait_ge(var, value)
                eng.tensor_tensor(st[0:ROWS, 1, :], st[0:ROWS, 0, :], minus_half[0:ROWS, :],
                                  ALU.pow).then_inc(rstd_, 1)

            def wide(v):
                return v.unsqueeze(2).to_broadcast([ROWS, GP, D])

            def row(v):
                return v.unsqueeze(1).to_broadcast([ROWS, GP, D])

            pool.wait_ge(rows_loaded, 64)

            def turn(g, project, attend, experts):
                ahead, now, last, before = counts(pool, g)
                if not since(g, 0):
                    rstd(st1, y_var, y_rstd, 1)
                    rstd(st2, h_var, h_rstd, 1)
                elif project:
                    pool.wait_ge(y_added, ahead)
                    eng.tensor_tensor(y_g[0:ROWS], y_c[0:ROWS], row(gamma_sb[0:ROWS, :]),
                                      ALU.mult).then_inc(y_scaled, 1)
                    rstd(st1, y_var, y_rstd, ahead)
                    pool.wait_ge(y_scaled, ahead)
                    pool.wait_ge(y_rstd, ahead)
                    eng.tensor_tensor(y_n[0:ROWS], y_g[0:ROWS], wide(st1[0:ROWS, 1, :]),
                                      ALU.mult).then_inc(y_normed, 1)
                    pool.wait_ge(y_normed, ahead)
                    pool.wait_ge(h_kept, now)
                    eng.tensor_tensor(h[0:ROWS, :, 0:D], y_n[0:ROWS], row(beta_sb[0:ROWS, :]), ALU.add
                                      ).then_inc(h_ready, 1)
                    rstd(st2, h_var, h_rstd, ahead)
                    pool.wait_ge(h_rstd, ahead)
                    pool.wait_ge(s_in_psum, now)
                    pool.wait_ge(s_tok_made, now)
                    eng.tensor_tensor(s[0:ROWS, 0:GP], h_c[0:ROWS], wide(st2[0:ROWS, 1, :]),
                                      ALU.mult).then_inc(s_ready, 1)
                if attend:
                    rstd(st3, a_var, a_rstd, now)

            turns(pool, turn)

        @block.scalar
        def _(act):
            eng = nc.scalar
            act.dma_start(tokw_raw[:], tok_w).then_inc(tokw_loaded, 16)
            for dst, src in ((tokb_sb, tok_b), (gamma_sb, tok_gamma), (beta_sb, tok_beta), (rb2_sb, router_b2)):
                act.dma_start(dst[:], src.partition_broadcast(128)).then_inc(rows_loaded, 16)
            act.dma_start(e_raw[:].rearrange("i (h j) -> i h j", h=HEADS),
                          attn_e.rearrange("h i j -> i h j")).then_inc(e_loaded, 16)

            def turn(g, project, attend, experts):
                ahead, now, last, before = counts(act, g)

                def qs_copy(i):
                    act.wait_ge(qs_in_psum[i], now)
                    if i == 0 and since(g, 1):
                        act.wait_ge(om_in_psum[GP - 1], last)
                    eng.copy(qs[:, :, i, :], ring[i % 2][:, 0:N].rearrange("p (c t) -> p c t", c=GC)
                             ).then_inc(qs_copied[i], 1)

                def z_copy(i):
                    act.wait_ge(z_in_psum[i], now)
                    if i == 0 and since(g, 1):
                        act.wait_ge(r_in_psum, last)
                    eng.copy(z_t[:, :, i, :].rearrange("p h (s u) -> p s h u", s=2)[:, :, :, 0:T],
                             zb[i % 2][:, 0:2 * HP * T].rearrange("p (s h t) -> p s h t", s=2, h=HP)
                             ).then_inc(z_copied[i], 1)

                def h1_relu(e):
                    act.wait_ge(h1_in_psum[e], last)
                    if since(g, 2):
                        act.wait_ge(h2_in_psum[e], before)
                    eng.activation(h1[:, e, :], ring[e % 2][:, 0:N], ACT.Relu,
                                   bias=b1_sb[:, e:e + 1]).then_inc(h1_made[e], 1)

                def h2_relu(e):
                    act.wait_ge(h2_in_psum[e], last)
                    if since(g, 2):
                        act.wait_ge(h2_weighted[e], before)
                    eng.activation(h2[:, e, :], ring[(e + 1) % 2][:, 0:N], ACT.Relu,
                                   bias=b2_sb[:, e:e + 1]).then_inc(h2_made[e], 1)

                def x_copy(value):
                    act.wait_ge(x_in_psum, value)
                    act.wait_ge(y_in_psum, value - 1 if isinstance(value, int) else now)
                    eng.copy(x_t[:], pairs_of(tb, BROWS)).then_inc(x_copied, 1)

                if attend:
                    qs_copy(0)
                if experts:
                    act.wait_ge(rh_in_psum, last)
                    if since(g, 2):
                        act.wait_ge(l_in_psum, before)
                    if not since(g, 2):
                        act.wait_ge(rest_loaded, 15 * 16)
                    eng.activation(rh[:, :, 0:T], tb[0:RHID, 0:N].rearrange("p (c t) -> p c t", c=GC),
                                   ACT.Relu, bias=rb1_sb[:, 0:1]).then_inc(rh_made, 1)
                if attend:
                    qs_copy(2)
                if project and since(g, 1):
                    x_copy(ahead)
                if experts:
                    h1_relu(0)
                    h1_relu(1)
                if project:
                    act.wait_ge(y_added, ahead)
                    eng.activation(y_sq[0:ROWS, :, 0:D], y_c[0:ROWS], ACT.Square, scale=D ** -0.5
                                   ).then_inc(y_squared, 1)
                if not since(g, 0):
                    x_copy(2)
                if experts:
                    h1_relu(2)
                    act.wait_ge(l_centred, last)
                    eng.activation(ex[0:ROWS], logits_c[0:ROWS], ACT.Exp).then_inc(ex_made, 1)
                if attend:
                    z_copy(0)
                    z_copy(1)
                elif experts:
                    h2_relu(0)
                if experts:
                    act.wait_ge(probs_made, last)
                    eng.activation(ex2[0:ROWS], probs[0:ROWS], ACT.Exp).then_inc(ex2_made, 1)
                if attend:
                    z_copy(2)
                    z_copy(3)
                if project:
                    act.wait_ge(h_centred, ahead)
                    eng.activation(h_sq[0:ROWS, :, 0:D], h_c[0:ROWS], ACT.Square, scale=D ** -0.5).then_inc(h_squared, 1)
                if experts:
                    if not attend:
                        h2_relu(1)
                        h2_relu(2)
                    act.wait_ge(gt_in_psum, last)
                    if since(g, 2):
                        act.wait_ge(o_in_psum, before)
                    eng.copy(gate_t[:, 0:ROWS + 1], tb[:, 0:ROWS + 1]).then_inc(gt_copied, 1)
                if experts and attend:
                    h2_relu(0)
                if attend:
                    act.wait_ge(a_centred, now)
                    eng.activation(a_sq[0:ROWS, :, 0:D], a_c[0:ROWS], ACT.Square, scale=D ** -0.5).then_inc(a_squared, 1)
                if experts and attend:
                    h2_relu(1)
                    h2_relu(2)
                if project:
                    if not since(g, 0):
                        act.wait_ge(cleared, 10)
                    act.wait_ge(s_in_psum, ahead)
                    if since(g, 0):
                        act.wait_ge(qs_in_psum[HP - 1], now)
                        act.wait_ge(om_in_psum[GP - 1], now)
                    eng.copy(s_split[0:64], clips_of(tb)[0:64]).then_inc(s_upper, 1)
                    eng.copy(s_feat[0:64, :, 0:T], clips_of(tb)[0:64]).then_inc(s_feat_top, 1)
                    eng.copy(s_feat[64:128, :, 64:64 + T], clips_of(tb)[0:64]).then_inc(s_feat_made, 1)
                if attend:
                    act.wait_ge(a_in_psum, now)
                    if since(g, 1):
                        act.wait_ge(h1_in_psum[EP - 1], last)
                    eng.copy(h_split[0:64], clips_of(tb)[0:64]).then_inc(a_upper, 1)

            turns(act, turn)

        @block.vector
        def _(dve):
            eng = nc.vector
            eng.memset(xin[:], 0.0).then_inc(xin_cleared, 1)
            dve.wait_ge(w_in_psum, 1)
            eng.tensor_copy(tokw_whole[:], yb[:, 0:2 * D].rearrange("p (h i) -> p h i", h=2)).then_inc(w_copied, 1)
            dve.wait_ge(w_copied, 1)
            eng.tensor_reduce(w_sums[:, 0:2], tokw_whole[:], axis=AX.X, op=ALU.add).then_inc(w_summed, 1)
            dve.wait_ge(w_summed, 1)
            eng.scalar_tensor_tensor(tokw_t[:], w_sums[:, 0:2].unsqueeze(2).to_broadcast([128, 2, D]), -1.0 / D,
                                     tokw_whole[:], ALU.mult, ALU.add).then_inc(w_centred, 1)
            dve.wait_ge(x_in_psum, 1)
            eng.tensor_copy(x_t[:], pairs_of(tb, BROWS)).then_inc(x_copied, 1)
            for tile in (y_sq, h_sq, a_sq):
                eng.memset(tile[:], EPS).then_inc(cleared, 1)
            dve.wait_ge(rows_loaded, 64)
            eng.tensor_reduce(w_sums[:, 2:3], tokb_sb[:].unsqueeze(1), axis=AX.X, op=ALU.add).then_inc(w_summed, 1)
            dve.wait_ge(w_summed, 2)
            eng.scalar_tensor_tensor(tokb_c[:], w_sums[:, 2:3].to_broadcast([128, D]), -1.0 / D, tokb_sb[:],
                                     ALU.mult, ALU.add).then_inc(w_centred, 1)
            for tile in (s_feat, rh, gate_parts, b3_raw, w2_diag, s, a_n):
                eng.memset(tile[:], 0.0).then_inc(cleared, 1)
            dve.wait_ge(half_mask, 1)
            eng.tensor_copy(causal[64:128, :], causal[0:64, :]).then_inc(mask_made, 1)
            dve.wait_ge(cleared, 13)
            dve.wait_ge(w_centred, 2)

            def split_weights():
                dve.wait_ge(e_in_psum, 1)
                e_ps = ring[0][:, 0:HP * D].rearrange("p (h i) -> p h i", h=HP)
                eng.tensor_copy(e_t[:, :, 0:D], e_ps).then_inc(e_copied, 1)
                eng.tensor_reduce(e_t[:, :, D], e_ps, axis=AX.X, op=ALU.add).then_inc(e_copied, 1)
                dve.wait_ge(q_loaded, 6 * 16)
                for k, (raw, hi) in enumerate(((q_raw, q_hi), (w1_raw, w1_hi), (rw1_raw, rw1_hi))):
                    eng.tensor_copy(hi[:], raw[:]).then_inc(q_rounded, 1)
                for k, (raw, hi, lo) in enumerate(((q_raw, q_hi, q_lo), (w1_raw, w1_hi, w1_lo),
                                                   (rw1_raw, rw1_hi, rw1_lo))):
                    dve.wait_ge(q_rounded, k + 1)
                    eng.tensor_tensor(lo[:], raw[:], hi[:].bitcast(F32), ALU.subtract).then_inc(q_split, 1)
                dve.wait_ge(spread_made, 1)
                eng.tensor_copy(spread[:].rearrange("p a e m -> p (a e m)"), spread_raw[:]).then_inc(spread_rounded, 1)
                dve.wait_ge(rest_loaded, 15 * 16)
                eng.tensor_copy(b3_hi[:], b3_raw[:]).then_inc(q_rounded, 1)
                dve.wait_ge(q_rounded, 4)
                eng.tensor_tensor(b3_lo[:], b3_raw[:], b3_hi[:].bitcast(F32), ALU.subtract).then_inc(q_split, 1)

            def row(v, n):
                return v.unsqueeze(1).to_broadcast([ROWS, GP, n])

            def wide(v, n):
                return v.unsqueeze(2).to_broadcast([ROWS, GP, n])

            def sum_rows(out_, in_, done):
                eng.tensor_reduce(out_, in_, axis=AX.X, op=ALU.add).then_inc(done, 1)

            def centre(out_, in_, sums, done):
                eng.scalar_tensor_tensor(out_, wide(sums, D), -1.0 / D, in_, ALU.mult, ALU.add).then_inc(done, 1)

            def turn(g, project, attend, experts):
                ahead, now, last, before = counts(dve, g)

                def h_of(k, width=D + 1):
                    return hbuf[0:ROWS, bass.ds(k, 1), :, 0:width].rearrange("p g a d -> p (g a) d")

                def mask(i):
                    dve.wait_ge(om_in_psum[i], now)
                    if since(g, 1):
                        dve.wait_ge(z_in_psum[i], last)
                    eng.tensor_tensor(omega[0:ROWS, 2 * i:2 * i + 2, :, :].rearrange("p c h t -> p (c h t)"),
                                      om[i % 2][0:ROWS, 0:N], causal[0:ROWS, :], ALU.mult).then_inc(om_masked[i], 1)

                def weigh(e):
                    dve.wait_ge(h2_made[e], last)
                    dve.wait_ge(gate_in_psum[e], last)
                    if e == 0 and since(g, 2):
                        dve.wait_ge(o_in_psum, before)
                    eng.tensor_tensor(h2w[:, e, :, 0:T], clips_of(zb[e % 2]),
                                      h2[:, e, :].rearrange("p (c t) -> p c t", c=GC),
                                      ALU.mult).then_inc(h2_weighted[e], 1)

                if attend:
                    for i in (1, 3):
                        dve.wait_ge(qs_in_psum[i], now)
                        if i == 1 and since(g, 1):
                            dve.wait_ge(om_in_psum[GP - 1], last)
                        eng.tensor_copy(qs[:, :, i, :], ring[i % 2][:, 0:N].rearrange("p (c t) -> p c t", c=GC)
                                        ).then_inc(qs_copied[i], 1)
                if project:
                    dve.wait_ge(y_in_psum, ahead)
                    if since(g, 0):
                        dve.wait_ge(y_scaled, now)
                    eng.tensor_tensor(y_c[0:ROWS], y_ps[0:ROWS], row(tokb_c[0:ROWS, :], D),
                                      ALU.add).then_inc(y_added, 1)
                if not since(g, 0):
                    dve.wait_ge(y_added, 1)
                    eng.tensor_tensor(y_g[0:ROWS], y_c[0:ROWS], row(gamma_sb[0:ROWS, :], D),
                                      ALU.mult).then_inc(y_scaled, 1)
                if attend:
                    mask(0)
                if experts:
                    dve.wait_ge(l_in_psum, last)
                    eng.tensor_tensor(logits[0:ROWS], l_ps[0:ROWS], row(rb2_sb[0:ROWS, :], EXPERTS),
                                      ALU.add).then_inc(l_added, 1)
                    dve.wait_ge(l_added, last)
                    eng.tensor_reduce(rst[0:ROWS, 0, :], logits[0:ROWS], axis=AX.X, op=ALU.max).then_inc(l_max, 1)
                if project:
                    dve.wait_ge(y_squared, ahead)
                    sum_rows(st1[0:ROWS, 0, :], y_sq[0:ROWS], y_var)
                if experts:
                    dve.wait_ge(l_max, last)
                    eng.tensor_tensor(logits_c[0:ROWS], logits[0:ROWS], wide(rst[0:ROWS, 0, :], EXPERTS),
                                      ALU.subtract).then_inc(l_centred, 1)
                if not since(g, 0):
                    split_weights()
                    dve.wait_ge(y_rstd, 1)
                    eng.tensor_tensor(y_n[0:ROWS], y_g[0:ROWS], wide(st1[0:ROWS, 1, :], D),
                                      ALU.mult).then_inc(y_normed, 1)
                    dve.wait_ge(y_normed, 1)
                    eng.tensor_tensor(h[0:ROWS, :, 0:D], y_n[0:ROWS], row(beta_sb[0:ROWS, :], D),
                                      ALU.add).then_inc(h_ready, 1)
                if attend:
                    mask(1)
                if experts:
                    dve.wait_ge(ex_made, last)
                    sum_rows(rst[0:ROWS, 1, :], ex[0:ROWS], ex_summed)
                    dve.wait_ge(ex_summed, last)
                    eng.reciprocal(rst[0:ROWS, 2, :], rst[0:ROWS, 1, :]).then_inc(ex_inv, 1)
                    dve.wait_ge(ex_inv, last)
                    eng.tensor_tensor(probs[0:ROWS], ex[0:ROWS], wide(rst[0:ROWS, 2, :], EXPERTS),
                                      ALU.mult).then_inc(probs_made, 1)
                if attend:
                    mask(2)
                if experts:
                    shape = [ROWS, GP, EXPERTS, EXPERTS]
                    other = probs[0:ROWS].unsqueeze(2).to_broadcast(shape)
                    own = probs[0:ROWS].unsqueeze(3).to_broadcast(shape)
                    dve.wait_ge(probs_made, last)
                    eng.tensor_tensor(above[0:ROWS], other, own, ALU.is_gt).then_inc(above_made, 1)
                    eng.tensor_tensor(tied[0:ROWS], other, own, ALU.is_ge).then_inc(tied_made, 1)
                if attend:
                    mask(3)
                if experts:
                    dve.wait_ge(tied_made, last)
                    eng.tensor_tensor(tied_e[0:ROWS], tied[0:ROWS],
                                      earlier[0:ROWS].unsqueeze(1).to_broadcast(shape), ALU.mult).then_inc(tied_cut, 1)
                    dve.wait_ge(above_made, last)
                    dve.wait_ge(tied_cut, last)
                    eng.tensor_tensor(beats[0:ROWS], above[0:ROWS], tied_e[0:ROWS], ALU.max).then_inc(beats_made, 1)
                    dve.wait_ge(beats_made, last)
                    eng.tensor_reduce(rank[0:ROWS], beats[0:ROWS], axis=AX.X, op=ALU.add).then_inc(rank_made, 1)
                    dve.wait_ge(rank_made, last)
                    dve.wait_ge(ex2_made, last)
                    eng.scalar_tensor_tensor(picked[0:ROWS], rank[0:ROWS], 1.5, ex2[0:ROWS], ALU.is_lt,
                                             ALU.mult).then_inc(picked_made, 1)
                    dve.wait_ge(picked_made, last)
                    sum_rows(rst[0:ROWS, 3, :], picked[0:ROWS], picked_sum)
                if project:
                    dve.wait_ge(h_ready, ahead)
                    sum_rows(h[0:ROWS, :, D], h[0:ROWS, :, 0:D], h_summed)
                if experts:
                    dve.wait_ge(picked_sum, last)
                    eng.reciprocal(rst[0:ROWS, 4, :], rst[0:ROWS, 3, :]).then_inc(picked_inv, 1)
                if project:
                    dve.wait_ge(h_summed, ahead)
                    if since(g, 0):
                        dve.wait_ge(s_ready, now)
                    centre(h_c[0:ROWS], h[0:ROWS, :, 0:D], h[0:ROWS, :, D], h_centred)
                    eng.tensor_copy(h_of(g + 1), h[0:ROWS]).then_inc(h_kept, 1)
                if experts:
                    dve.wait_ge(picked_inv, last)
                    eng.tensor_tensor(gate[0:ROWS], picked[0:ROWS], wide(rst[0:ROWS, 4, :], EXPERTS),
                                      ALU.mult).then_inc(gate_made, 1)
                    dve.wait_ge(gate_made, last)
                    if since(g, 2):
                        dve.wait_ge(gt_in_psum, before)
                    eng.tensor_copy(gate_up[0:ROWS].bitcast(F32R), gate[0:ROWS]).then_inc(gate_upper, 1)
                    dve.wait_ge(gate_upper, last)
                    eng.tensor_tensor(gate_low[0:ROWS], gate[0:ROWS], gate_up[0:ROWS], ALU.subtract).then_inc(gate_split, 1)
                if project:
                    dve.wait_ge(h_squared, ahead)
                    sum_rows(st2[0:ROWS, 0, :], h_sq[0:ROWS], h_var)
                if not since(g, 0):
                    dve.wait_ge(h_rstd, 1)
                    eng.tensor_tensor(s[0:ROWS, 0:GP], h_c[0:ROWS], wide(st2[0:ROWS, 1, :], D),
                                      ALU.mult).then_inc(s_ready, 1)
                if attend:
                    dve.wait_ge(r_in_psum, now)
                    dve.wait_ge(h_kept, now)
                    eng.tensor_tensor(a[0:ROWS], r_ps[0:ROWS], h_of(g), ALU.add).then_inc(a_ready, 1)
                    dve.wait_ge(a_ready, now)
                    centre(a_c[0:ROWS], a[0:ROWS, :, 0:D], a[0:ROWS, :, D], a_centred)
                    eng.tensor_copy(h_of(g, D), a[0:ROWS, :, 0:D]).then_inc(a_kept, 1)
                if experts:
                    weigh(0)
                if attend:
                    dve.wait_ge(a_squared, now)
                    sum_rows(st3[0:ROWS, 0, :], a_sq[0:ROWS], a_var)
                if experts:
                    weigh(1)
                if attend:
                    dve.wait_ge(a_rstd, now)
                    if since(g, 1):
                        dve.wait_ge(a_in_psum, last)
                    eng.tensor_tensor(a_n[0:ROWS, 0:GP], a_c[0:ROWS], wide(st3[0:ROWS, 1, :], D),
                                      ALU.mult).then_inc(a_normed, 1)
                if experts:
                    weigh(2)
                if project:
                    dve.wait_ge(s_ready, ahead)
                    if since(g, 0):
                        dve.wait_ge(z_in_psum[GP - 1], now)
                    for side in range(2):
                        for par in range(2):
                            last_copy = eng.tensor_copy(
                                s_tok[64 * par:64 * par + T, :, 64 * par:64 * par + D].rearrange(
                                    "p (a c) d -> p a c d", c=2)[:, :, side, :],
                                s[64 * side:64 * side + T, 0:GP, :])
                    last_copy.then_inc(s_tok_made, 1)
                    dve.wait_ge(s_feat_made, ahead)
                    dve.wait_ge(s_upper, ahead)
                    eng.tensor_tensor(s_split[64:128], clips_of(tb)[0:64], s_split[0:64].bitcast(F32),
                                      ALU.subtract).then_inc(s_split_made, 1)
                if attend:
                    dve.wait_ge(a_upper, now)
                    eng.tensor_tensor(h_split[64:128], clips_of(tb)[0:64], h_split[0:64].bitcast(F32),
                                      ALU.subtract).then_inc(a_split_made, 1)
                if experts:
                    dve.wait_ge(o_in_psum, last)
                    dve.wait_ge(a_kept, last)
                    eng.tensor_tensor(h_of(g - 1, D), y_ps[0:ROWS], h_of(g - 1, D), ALU.add).then_inc(o_added, 1)

            turns(dve, turn)

        @block.tensor
        def _(pe):
            mm, tr = nc.tensor.matmul, nc.tensor.transpose
            pe.wait_ge(consts, 1)
            pe.wait_ge(tokw_loaded, 16)
            for half in range(2):
                done = tr(yb[0:128, D * half:D * (half + 1)], tokw_raw[:, BLK * half:BLK * (half + 1)],
                          ident[0:D, 0:D])
            done.then_inc(w_in_psum, 1)

            def split_matmul(out_, hi, lo, moving):
                mm(out_, hi, moving, start=True, stop=False)
                return mm(out_, lo, moving, start=False, stop=True)

            def turn(g, project, attend, experts):
                ahead, now, last, before = counts(pe, g)

                def qs_product(i):
                    if i == 0:
                        pe.wait_ge(s_split_made, now)
                        if since(g, 1):
                            pe.wait_ge(h2_made[EP - 1], before)
                    if i >= 2:
                        pe.wait_ge(qs_copied[i - 2], now)
                    split_matmul(ring[i % 2][:, 0:N], q_hi[:, i, :], q_lo[:, i, :],
                                 s_split[:].rearrange("p c t -> p (c t)")).then_inc(qs_in_psum[i], 1)

                def omega_product(i):
                    if i == 0:
                        pe.wait_ge(qs_copied[HP - 2], now)
                        pe.wait_ge(qs_copied[HP - 1], now)
                        pe.wait_ge(s_feat_made, now)
                    if i >= 2:
                        pe.wait_ge(om_masked[i - 2], now)
                    elif since(g, 1):
                        pe.wait_ge(om_masked[i + 2], last)
                    for c in range(2):
                        done = mm(om[i % 2][0:ROWS, HP * T * c:HP * T * (c + 1)], s_feat[:, 2 * i + c, 0:ROWS],
                                  qs[:, 2 * i + c, :, :].rearrange("p h t -> p (h t)"), start=True, stop=True)
                    done.then_inc(om_in_psum[i], 1)

                def z_product(i):
                    pe.wait_ge(om_masked[i], now)
                    if i == 0:
                        pe.wait_ge(s_tok_made, now)
                        if since(g, 2):
                            pe.wait_ge(h2_weighted[2], before)
                    elif i == 1 and since(g, 2):
                        pe.wait_ge(h2_weighted[1], before)
                    elif i >= 2:
                        pe.wait_ge(z_copied[i - 2], now)
                    for c in range(2):
                        done = mm(zb[i % 2][:, HP * T * c:HP * T * (c + 1)], s_tok[0:ROWS, 2 * i + c, :],
                                  omega[0:ROWS, 2 * i + c, :, :].rearrange("p h t -> p (h t)"), start=True, stop=True)
                    done.then_inc(z_in_psum[i], 1)

                def gate_spread(e):
                    if e == 0:
                        pe.wait_ge(gt_copied, last)
                    if e == 2:
                        pe.wait_ge(h2_weighted[0], last)
                    elif attend:
                        pe.wait_ge(z_copied[2 + e], now)
                    else:
                        pe.wait_ge(h2_weighted[2 - e], before)
                    for p in range(GP):
                        done = mm(zb[e % 2][:, 128 * p:128 * p + ROWS + 1], spread[:, p, e, :], gate_t[:, 0:ROWS + 1],
                                  start=True, stop=True)
                    done.then_inc(gate_in_psum[e], 1)

                def h1_product(e):
                    if e == 2:
                        pe.wait_ge(h1_made[0], last)
                    elif attend:
                        pe.wait_ge(qs_copied[2 + e], now)
                    elif e == 0:
                        pe.wait_ge(h2_made[EP - 1], before)
                    split_matmul(ring[e % 2][:, 0:N], w1_hi[:, e, :], w1_lo[:, e, :],
                                 h_split[:].rearrange("p c t -> p (c t)")).then_inc(h1_in_psum[e], 1)

                def head_sum(p):
                    pe.wait_ge(z_copied[p], now)
                    if p == 0 and experts:
                        pe.wait_ge(l_added, last)
                    elif p == 0:
                        pe.wait_ge(y_added, ahead)
                    for i in range(HP):
                        done = mm(yb[0:ROWS, (D + 1) * p:(D + 1) * (p + 1)], z_t[:, i, p, 0:ROWS], e_t[:, i, :],
                                  start=i == 0, stop=i == HP - 1)
                    return done

                def last_layer(e):
                    pe.wait_ge(h2_weighted[e], last)
                    for p in range(GP):
                        done = mm(yb[0:ROWS, D * p:D * (p + 1)],
                                  h2w[:, e, 2 * p:2 * p + 2, :].rearrange("p c u -> p (c u)")[:, 0:ROWS],
                                  w3_sb[:, e, :], start=e == 0 and p == 0, stop=e == EP - 1,
                                  skip_group_check=True)
                    return done

                def h2_product(e):
                    pe.wait_ge(h1_made[e], last)
                    if e < 2:
                        pe.wait_ge(h1_made[e + 1], last)
                    else:
                        pe.wait_ge(h2_made[0], last)
                    mm(ring[(e + 1) % 2][:, 0:N], w2_diag[:, e, :], h1[:, e, :], start=True,
                       stop=True).then_inc(h2_in_psum[e], 1)

                def x_transposes(value):
                    pe.wait_ge(x_loaded, 32 * value)
                    for p in range(GP):
                        done = tr(tb[:, 128 * p:128 * p + BROWS], xin[0:BROWS, p, :], ident[0:BROWS, 0:BROWS])
                    done.then_inc(x_in_psum, 1)

                def y_products(value):
                    pe.wait_ge(x_copied, value)
                    for p in range(GP):
                        for half in range(2):
                            done = mm(yb[0:ROWS, D * p:D * (p + 1)], x_t[:, p, half:half + ROWS],
                                      tokw_t[:, half, :], start=half == 0, stop=half == 1)
                    done.then_inc(y_in_psum, 1)

                if attend:
                    if not since(g, 1):
                        pe.wait_ge(e_copied, 2)
                        pe.wait_ge(q_split, 4)
                        pe.wait_ge(spread_rounded, 1)
                    qs_product(0)
                    qs_product(1)
                if experts:
                    pe.wait_ge(a_split_made, last)
                    split_matmul(tb[0:RHID, 0:N], rw1_hi[:], rw1_lo[:],
                                 h_split[:].rearrange("p c t -> p (c t)")).then_inc(rh_in_psum, 1)
                if attend:
                    qs_product(2)
                    qs_product(3)
                if project and since(g, 1):
                    pe.wait_ge(rh_made, last)
                    x_transposes(ahead)
                elif not since(g, 0):
                    x_transposes(1)
                if experts:
                    h1_product(0)
                    h1_product(1)
                if project and since(g, 1):
                    if since(g, 2):
                        pe.wait_ge(o_added, before)
                    y_products(ahead)
                elif not since(g, 0):
                    pe.wait_ge(w_centred, 1)
                    y_products(1)
                    pe.wait_ge(e_loaded, 16)
                    for i in range(HP):
                        done = tr(ring[0][:, D * i:D * (i + 1)], e_raw[:, 128 * i:128 * (i + 1)], ident[0:D, 0:D])
                    done.then_inc(e_in_psum, 1)
                    x_transposes(2)
                    pe.wait_ge(y_added, 1)
                    y_products(2)
                if attend:
                    omega_product(0)
                if experts:
                    pe.wait_ge(rh_made, last)
                    if project:
                        pe.wait_ge(y_added, ahead)
                    else:
                        pe.wait_ge(o_added, before)
                    for p in range(GP):
                        done = mm(yb[0:ROWS, EXPERTS * p:EXPERTS * (p + 1)],
                                  rh[:, 2 * p:2 * p + 2, :].rearrange("p c u -> p (c u)")[:, 0:ROWS], rw2_sb[:],
                                  start=True, stop=True)
                    done.then_inc(l_in_psum, 1)
                if attend:
                    omega_product(1)
                if experts:
                    h1_product(2)
                if attend:
                    z_product(0)
                    omega_product(2)
                    z_product(1)
                    omega_product(3)
                    z_product(2)
                    head_sum(0)
                    z_product(3)
                    head_sum(1)
                    head_sum(2)
                    head_sum(3).then_inc(r_in_psum, 1)
                elif experts:
                    h2_product(0)
                    h2_product(1)
                    h2_product(2)
                if experts:
                    pe.wait_ge(gate_split, last)
                    if project:
                        pe.wait_ge(x_copied, ahead)
                    else:
                        pe.wait_ge(rh_made, last)
                    tr(tb[:, 0:ROWS + 1], gate_parts[0:ROWS + 1, :], ident[0:ROWS + 1, 0:ROWS + 1]
                       ).then_inc(gt_in_psum, 1)
                    for e in range(EP):
                        if attend:
                            h2_product(e)
                        gate_spread(e)
                if project:
                    pe.wait_ge(s_ready, ahead)
                    if experts:
                        pe.wait_ge(gt_copied, last)
                    elif attend:
                        pe.wait_ge(s_split_made, now)
                    else:
                        pe.wait_ge(x_copied, 2)
                    for p in range(GP):
                        done = tr(tb[:, 128 * p:128 * p + ROWS], s[0:ROWS, p:p + 2, :].rearrange("p a d -> p (a d)"), ident[0:ROWS, 0:ROWS])
                    done.then_inc(s_in_psum, 1)
                if experts:
                    if attend:
                        pe.wait_ge(a_ready, now)
                    else:
                        pe.wait_ge(l_added, last)
                    last_layer(0)
                    last_layer(1)
                    for p in range(GP):
                        for part in (b3_hi, b3_lo):
                            mm(yb[0:ROWS, D * p:D * (p + 1)], gate_t[:, 0:ROWS], part[:, p, :], start=False,
                               stop=False, skip_group_check=True)
                if attend:
                    pe.wait_ge(a_normed, now)
                    if project:
                        pe.wait_ge(s_split_made, ahead)
                    elif experts:
                        pe.wait_ge(gt_copied, last)
                    for p in range(GP):
                        done = tr(tb[:, 128 * p:128 * p + ROWS], a_n[0:ROWS, p:p + 2, :].rearrange("p a d -> p (a d)"), ident[0:ROWS, 0:ROWS])
                    done.then_inc(a_in_psum, 1)
                if experts:
                    last_layer(2).then_inc(o_in_psum, 1)

            turns(pe, turn)


_INS = ['x', 'L0_tok_W', 'L0_tok_b', 'L0_tok_gamma', 'L0_tok_beta', 'L0_attn_Q', 'L0_attn_E',
        'L0_ffn_router_w1', 'L0_ffn_router_b1', 'L0_ffn_router_w2', 'L0_ffn_router_b2',
        'L0_ffn_expert_w1', 'L0_ffn_expert_b1', 'L0_ffn_expert_w2', 'L0_ffn_expert_b2',
        'L0_ffn_expert_w3', 'L0_ffn_expert_b3']
_OUTS = [((64, 45, 64), 'float32')]


def kernel(**inputs):
    import numpy as _np
    import concourse.bacc as _bacc
    from concourse import mybir as _mybir
    from concourse.bass_utils import run_bass_kernel_spmd as _run

    nc = _bacc.Bacc("TRN2", target_bir_lowering=False, num_devices=1)
    arrays, args = {}, []
    for name in _INS:
        a = _np.ascontiguousarray(inputs[name])
        arrays[f"in_{name}_dram"] = a
        args.append(nc.dram_tensor(f"in_{name}_dram", a.shape, _mybir.dt.from_np(a.dtype), kind="ExternalInput").ap())
    for i, (shape, dtype) in enumerate(_OUTS):
        dt = _mybir.dt.from_np(_np.dtype(dtype))
        args.append(nc.dram_tensor(f"out_{i}_dram", shape, dt, kind="ExternalOutput").ap())
    audio_tower(nc, *args)
    r = _run(nc, [arrays], core_ids=[0])
    got = tuple(r.results[0][f"out_{i}_dram"] for i in range(len(_OUTS)))
    return got[0]
```

```python
import concourse.bass as bass
from concourse import mybir
from contextlib import ExitStack



def audio_tower(nc, x, tok_w, tok_b, tok_gamma, tok_beta, attn_q, attn_e, router_w1, router_b1,
                router_w2, router_b2, w1, b1, w2, b2, w3, b3, out):
    F32, F32R = mybir.dt.float32, mybir.dt.float32r
    ALU, ACT, AX = mybir.AluOpType, mybir.ActivationFunctionType, mybir.AxisListType

    CLIPS, STEPS, FREQ = x.shape
    D, PATCH_IN = tok_w.shape
    HEADS = attn_q.shape[0]
    EXPERTS, _, HID = w1.shape
    RHID = router_w1.shape[1]
    T = out.shape[1]
    EPS = 1e-5
    BLK = PATCH_IN // 2
    NBLK = T + 1
    GC = 8
    GP = GC // 2
    G = CLIPS // GC
    N = GC * T
    ROWS = 64 + T
    BROWS = 64 + NBLK
    HP = HEADS // 2
    EP = EXPERTS // 2
    XCOLS = NBLK * BLK

    x_blocks = x.rearrange("b r f -> b (r f)")[:, 0:XCOLS].rearrange(
        "(p side) (k c) -> side k p c", side=2, c=BLK)
    out_rows = out.rearrange("(p side) t d -> side t p d", side=2)

    with ExitStack() as ctx:
        def sb(name, shape, dt=F32):
            return ctx.enter_context(nc.sbuf_tensor(name, shape, dt))

        def pb(name):
            return ctx.enter_context(nc.psum_tensor(name, [128, 512], F32))

        def sem(name):
            return ctx.enter_context(nc.semaphore(name))

        ident = sb("ident", [128, 128])
        causal = sb("causal", [128, N])
        earlier = sb("earlier", [128, EXPERTS, EXPERTS])
        minus_half = sb("minus_half", [128, GP])
        q_raw = sb("q_raw", [128, HP, 128])
        q_hi = sb("q_hi", [128, HP, 128], F32R)
        q_lo = sb("q_lo", [128, HP, 128], F32R)
        w1_raw = sb("w1_raw", [128, EP, 128])
        w1_hi = sb("w1_hi", [128, EP, 128], F32R)
        w1_lo = sb("w1_lo", [128, EP, 128], F32R)
        rw1_raw = sb("rw1_raw", [128, RHID])
        rw1_hi = sb("rw1_hi", [128, RHID], F32R)
        rw1_lo = sb("rw1_lo", [128, RHID], F32R)
        e_raw = sb("e_raw", [D, HEADS * D])
        tokw_raw = sb("tokw_raw", [D, PATCH_IN])
        e_t = sb("e_t", [128, HP, D])
        fold = sb("fold", [128, D + 1])
        tokw_whole = sb("tokw_whole", [128, 2, D])
        tokw_t = sb("tokw_t", [128, 2, D])
        tokb_c = sb("tokb_c", [128, D])
        w_sums = sb("w_sums", [128, 3])
        w2_diag = sb("w2_diag", [128, EP, 128])
        w3_sb = sb("w3_sb", [128, EP, D])
        w3_diag = sb("w3_diag", [128, EP, 2, D])
        b3_flat = sb("b3_flat", [64, EXPERTS * D])
        b3_rows = sb("b3_rows", [64, EXPERTS * D], F32R)
        ones_raw = sb("ones_raw", [64, 128])
        ones = sb("ones", [64, 128], F32R)
        rw2_sb = sb("rw2_sb", [RHID, EXPERTS])
        b1_sb = sb("b1_sb", [128, EP])
        b2_sb = sb("b2_sb", [128, EP])
        rb1_sb = sb("rb1_sb", [RHID, 1])
        b3_raw = sb("b3_raw", [128, D])
        b3_hi = sb("b3_hi", [128, D], F32R)
        b3_parts = sb("b3_parts", [128, D], F32R)
        spread_raw = sb("spread_raw", [128, EP * 128])
        spread = sb("spread", [128, EP, 128], F32R)
        tokb_sb = sb("tokb_sb", [128, D])
        gamma_sb = sb("gamma_sb", [128, D])
        beta_sb = sb("beta_sb", [128, D])
        rb2_sb = sb("rb2_sb", [128, EXPERTS])

        xin = sb("xin", [128, GP, BLK])
        x_t = sb("x_t", [128, GP, BROWS])
        y_c = sb("y_c", [128, GP, D])
        y_sq = sb("y_sq", [128, GP, D + 1])
        y_g = sb("y_g", [128, GP, D])
        y_n = sb("y_n", [128, GP, D])
        hbuf = sb("hbuf", [128, G, GP, D + 1])
        h_c = sb("h_c", [128, GP, D])
        h_sq = sb("h_sq", [128, GP, D + 1])
        h = sb("h", [128, GP, D + 1])
        s = sb("s", [128, GP + 1, D])
        st1 = sb("st1", [128, 2, GP])
        st2 = sb("st2", [128, 2, GP])
        st3 = sb("st3", [128, 2, GP])

        s_split = sb("s_split", [128, GC, T], F32R)
        s_feat = sb("s_feat", [128, GC, 128])
        s_tok = sb("s_tok", [128, GC, 128])
        qs = sb("qs", [128, GC, HP, T])
        omega = sb("omega", [128, GC, HP, T])
        z_t = sb("z_t", [128, HP, GC, T])
        r_t = sb("r_t", [128, GC, 64])
        a_c = sb("a_c", [128, GP, D])
        a_sq = sb("a_sq", [128, GP, D + 1])
        a = sb("a", [128, GP, D + 1])
        a_n = sb("a_n", [128, GP + 1, D])

        h_split = sb("h_split", [128, GC, T], F32R)
        rh = sb("rh", [RHID, GC, 64])
        logits = sb("logits", [128, GP, EXPERTS])
        logits_c = sb("logits_c", [128, GP, EXPERTS])
        ex = sb("ex", [128, GP, EXPERTS])
        probs = sb("probs", [128, GP, EXPERTS])
        ex2 = sb("ex2", [128, GP, EXPERTS])
        picked = sb("picked", [128, GP, EXPERTS])
        rank = sb("rank", [128, GP, EXPERTS])
        above = sb("above", [128, GP, EXPERTS, EXPERTS])
        tied = sb("tied", [128, GP, EXPERTS, EXPERTS])
        tied_e = sb("tied_e", [128, GP, EXPERTS, EXPERTS])
        beats = sb("beats", [128, GP, EXPERTS, EXPERTS])
        rst = sb("rst", [128, 5, GP])
        gate = sb("gate", [128, GP, EXPERTS])
        gate_parts = sb("gate_parts", [128, GP, 128])
        gate_t = sb("gate_t", [128, GC, 64], F32R)
        h1 = sb("h1", [128, EP, N])
        h2 = sb("h2", [128, EP, N])
        h2w = sb("h2w", [128, EP, GC, 64])
        outs = sb("outs", [128, EP, GP, 2 * D])
        gate_cols = gate_parts[:, :, 0:64].rearrange("p a (c k) -> p a c k", c=2)
        gate_up = gate_cols[0:ROWS, :, :, 0:EXPERTS]
        gate_low = gate_cols[0:ROWS, :, :, EXPERTS:2 * EXPERTS]

        ring = [pb("ring0"), pb("ring1")]
        om = [pb("om0"), pb("om1")]
        zb = [pb("zb0"), pb("zb1")]
        gates = [zb[0], zb[1], om[0]]
        tb = pb("tb")
        yb = pb("yb")

        gt_ps = om[1]

        def pairs_of(bank, width):
            return bank[:, :].rearrange("p (a c) -> p a c", a=GP)[:, :, 0:width]

        def clips_of(bank):
            return bank[:, :].rearrange("p (c u) -> p c u", u=64)[:, :, 0:T]

        def gates_of(bank):
            return bank[:, 0:GC * (T + 1)].rearrange("p (c u) -> p c u", c=GC)[:, :, 0:T]

        y_ps = om[0][:, 0:GP * D].rearrange("p (a d) -> p a d", a=GP)
        o_ps = yb[:, 0:GP * D].rearrange("p (a d) -> p a d", a=GP)
        r_ps = yb[:, 0:GP * (D + 1)].rearrange("p (a d) -> p a d", a=GP)
        l_ps = yb[:, 0:GP * EXPERTS].rearrange("p (a e) -> p a e", a=GP)

        x_loaded, stored = sem("x_loaded"), sem("stored")
        tokw_loaded, q_loaded, e_loaded, rows_loaded, rest_loaded = (
            sem(n) for n in ("tokw_loaded", "q_loaded", "e_loaded", "rows_loaded", "rest_loaded"))
        xin_cleared, cleared, consts = sem("xin_cleared"), sem("cleared"), sem("consts")
        weights_cleared = sem("weights_cleared")
        half_mask, mask_made = sem("half_mask"), sem("mask_made")
        pool_step = sem("pool_step")
        e_in_psum, e_copied = sem("e_in_psum"), sem("e_copied")
        w_in_psum, w_copied, w_summed, w_centred, q_rounded, q_split = (
            sem(n) for n in ("w_in_psum", "w_copied", "w_summed", "w_centred", "q_rounded", "q_split"))
        x_in_psum, x_copied, y_in_psum = sem("x_in_psum"), sem("x_copied"), sem("y_in_psum")
        y_added, y_squared, y_var = sem("y_added"), sem("y_squared"), sem("y_var")
        y_scaled, y_rstd, y_normed, h_ready = (sem(n) for n in ("y_scaled", "y_rstd", "y_normed", "h_ready"))
        h_summed, h_centred, h_squared, h_var, h_rstd, s_ready = (
            sem(n) for n in ("h_summed", "h_centred", "h_squared", "h_var", "h_rstd", "s_ready"))
        s_in_psum, s_upper, s_feat_top, s_feat_made, s_split_made, s_tok_made = (
            sem(n) for n in ("s_in_psum", "s_upper", "s_feat_top", "s_feat_made", "s_split_made", "s_tok_made"))
        qs_in_psum = [sem(f"qs_in_psum{i}") for i in range(HP)]
        qs_copied = [sem(f"qs_copied{i}") for i in range(HP)]
        om_in_psum = [sem(f"om_in_psum{i}") for i in range(GP)]
        om_masked = [sem(f"om_masked{i}") for i in range(GP)]
        z_in_psum = [sem(f"z_in_psum{i}") for i in range(GP)]
        z_copied = [sem(f"z_copied{i}") for i in range(GP)]
        rt_in_psum, rt_copied = sem("rt_in_psum"), sem("rt_copied")
        r_in_psum, a_ready, a_centred, a_squared, a_var, a_rstd, a_normed = (
            sem(n) for n in ("r_in_psum", "a_ready", "a_centred", "a_squared", "a_var", "a_rstd", "a_normed"))
        h_kept, a_kept = sem("h_kept"), sem("a_kept")
        a_in_psum, a_upper, a_split_made = sem("a_in_psum"), sem("a_upper"), sem("a_split_made")
        rh_in_psum, rh_made, l_in_psum, l_added, l_max, l_centred, ex_made = (
            sem(n) for n in ("rh_in_psum", "rh_made", "l_in_psum", "l_added", "l_max", "l_centred", "ex_made"))
        ex_summed, ex_inv, probs_made, ex2_made, above_made, tied_made, tied_cut, beats_made = (
            sem(n) for n in ("ex_summed", "ex_inv", "probs_made", "ex2_made", "above_made", "tied_made",
                             "tied_cut", "beats_made"))
        rank_made, picked_made, picked_sum, picked_inv, gate_made, gate_upper, gate_split = (
            sem(n) for n in ("rank_made", "picked_made", "picked_sum", "picked_inv", "gate_made",
                             "gate_upper", "gate_split"))
        fold_step = sem("fold_step")
        spread_made, spread_rounded = sem("spread_made"), sem("spread_rounded")
        h1_in_psum = [sem(f"h1_in_psum{i}") for i in range(EP)]
        h1_made = [sem(f"h1_made{i}") for i in range(EP)]
        gate_in_psum = [sem(f"gate_in_psum{i}") for i in range(EP)]
        h2_in_psum = [sem(f"h2_in_psum{i}") for i in range(EP)]
        h2_made = [sem(f"h2_made{i}") for i in range(EP)]
        outs_in_psum = [sem(f"outs_in_psum{i}") for i in range(EP)]
        outs_weighted = sem("outs_weighted")
        h2_weighted = [sem(f"h2_weighted{i}") for i in range(EP)]
        gt_in_psum, gt_copied, o_in_psum, o_added = (
            sem(n) for n in ("gt_in_psum", "gt_copied", "o_in_psum", "o_added"))

        block = ctx.enter_context(nc.Block())

        def counts(engine, g):
            if isinstance(g, int):
                return g + 2, g + 1, g, g - 1
            return engine.snap(g + 2), engine.snap(g + 1), g, engine.snap(g - 1)

        def turns(engine, turn):
            turn(-1, project=True, attend=False, experts=False)
            turn(0, project=True, attend=True, experts=False)
            turn(1, project=True, attend=True, experts=True)
            with engine.Fori(2, G - 2) as g:
                turn(g, project=True, attend=True, experts=True)
            turn(G - 2, project=True, attend=True, experts=True)
            turn(G - 1, project=False, attend=True, experts=True)
            turn(G, project=False, attend=False, experts=True)

        def since(g, least):
            return not isinstance(g, int) or g >= least

        def h_of(k, width=D + 1):
            return hbuf[0:ROWS, bass.ds(k, 1), :, 0:width].rearrange("p g a d -> p (g a) d")

        @block.sync
        def _(sp):
            sp.wait_ge(xin_cleared, 1)

            def load_blocks(group):
                for side in range(2):
                    sp.dma_start(xin[64 * side:64 * side + NBLK, :, :],
                                 x_blocks[side][:, bass.ds(group * GP, GP), :]).then_inc(x_loaded, 16)

            load_blocks(0)
            sp.wait_ge(x_in_psum, 1)
            load_blocks(1)
            for half in range(2):
                sp.dma_start(q_raw[64 * half:64 * half + D, :, :].rearrange("i p (s j) -> i (p s) j", s=2),
                             attn_q.rearrange("h i j -> i h j")).then_inc(q_loaded, 16)
            for half in range(2):
                rows = slice(64 * half, 64 * half + D)
                sp.dma_start(rw1_raw[rows, :], router_w1).then_inc(q_loaded, 16)
                sp.dma_start(w1_raw[rows, :, :].rearrange("d p (s h) -> d (p s) h", s=2),
                             w1.rearrange("e d h -> d e h")).then_inc(q_loaded, 16)
            sp.dma_start(rb1_sb[:], router_b1.unsqueeze(1)).then_inc(rest_loaded, 16)
            sp.dma_start(rw2_sb[:], router_w2).then_inc(rest_loaded, 16)
            sp.dma_start(b1_sb[:], b1.rearrange("(p s) h -> (s h) p", s=2),
                         allow_slow_non_contiguous=True).then_inc(rest_loaded, 16)
            sp.dma_start(b2_sb[:], b2.rearrange("(p s) h -> (s h) p", s=2),
                         allow_slow_non_contiguous=True).then_inc(rest_loaded, 16)
            sp.dma_start(w3_sb[:], w3.rearrange("(p s) f o -> (s f) p o", s=2)).then_inc(rest_loaded, 16)
            sp.wait_ge(weights_cleared, 4)
            for row in (0, 32):
                sp.dma_start(b3_flat[row:row + 1, :], b3.rearrange("e d -> (e d)").unsqueeze(0)
                             ).then_inc(rest_loaded, 16)
            for half in range(2):
                rows = slice(64 * half, 64 * half + HID)
                sp.dma_start(w2_diag[rows, :, rows],
                             w2.rearrange("(p s) h f -> s h p f", s=2)[half]).then_inc(rest_loaded, 16)
                sp.dma_start(w3_diag[rows, :, half, :],
                             w3.rearrange("(p s) f o -> s f p o", s=2)[half]).then_inc(rest_loaded, 16)
            for top in (0, EXPERTS, 32, 32 + EXPERTS):
                sp.dma_start(b3_raw[top:top + EXPERTS, :], b3).then_inc(rest_loaded, 16)

            def turn(g, project, attend, experts):
                ahead, now, last, before = counts(sp, g)
                if project and since(g, 0) and not (isinstance(g, int) and g == G - 2):
                    sp.wait_ge(x_in_psum, ahead)
                    load_blocks(g + 2)
                if experts:
                    sp.wait_ge(o_added, last)
                    for side in range(2):
                        sp.dma_start(out_rows[side][:, bass.ds(g * GP - GP, GP), :],
                                     hbuf[64 * side:64 * side + T, bass.ds(g - 1, 1), :, 0:D].rearrange(
                                         "p g a d -> p (g a) d")).then_inc(stored, 16)

            turns(sp, turn)
            sp.wait_ge(stored, 32 * G)

        @block.gpsimd
        def _(pool):
            eng = nc.gpsimd
            eng.memset(ident[:], 0.0).then_inc(pool_step, 1)
            pool.wait_ge(pool_step, 1)
            eng.affine_select(out=ident[:], in_=ident[:], compare_op=ALU.not_equal, fill=1.0, base=0,
                              pattern=[[-1, 128]], channel_multiplier=1).then_inc(consts, 1)
            eng.memset(minus_half[:], -0.5).then_inc(pool_step, 1)
            eng.memset(earlier[:], 1.0).then_inc(pool_step, 1)
            eng.memset(causal[:], 1.0).then_inc(pool_step, 1)
            pool.wait_ge(pool_step, 4)
            eng.affine_select(out=causal[0:64, :].rearrange("p (c t) -> p c t", c=GC),
                              in_=causal[0:64, :].rearrange("p (c t) -> p c t", c=GC),
                              compare_op=ALU.is_ge, fill=0.0, base=0, pattern=[[0, GC], [1, T]],
                              channel_multiplier=-1).then_inc(half_mask, 1)
            eng.affine_select(out=earlier[:], in_=earlier[:], compare_op=ALU.is_gt, fill=0.0, base=0,
                              pattern=[[1, EXPERTS], [-1, EXPERTS]], channel_multiplier=0).then_inc(consts, 1)
            eng.memset(spread_raw[:], 0.0).then_inc(pool_step, 1)
            for part in range(2):
                pool.wait_ge(pool_step, 5 + part)
                done = eng.affine_select(out=spread_raw[:], in_=spread_raw[:], compare_op=ALU.not_equal, fill=1.0,
                                         base=-EXPERTS * part, pattern=[[-2, EP], [-1, 2], [0, HID]],
                                         channel_multiplier=1)
                done.then_inc(pool_step if part == 0 else spread_made, 1)
            for tile in (w2_diag, w3_diag, b3_raw, b3_flat):
                eng.memset(tile[:], 0.0).then_inc(weights_cleared, 1)
            eng.memset(ones_raw[:], 1.0).then_inc(cleared, 1)
            for tile in (s_tok, r_t, h2w, rh, gate_parts, a_n):
                eng.memset(tile[:], 0.0).then_inc(cleared, 1)

            def rstd(st, var, rstd_, value):
                pool.wait_ge(var, value)
                eng.tensor_tensor(st[0:ROWS, 1, :], st[0:ROWS, 0, :], minus_half[0:ROWS, :],
                                  ALU.pow).then_inc(rstd_, 1)

            def wide(v):
                return v.unsqueeze(2).to_broadcast([ROWS, GP, D])

            def row(v):
                return v.unsqueeze(1).to_broadcast([ROWS, GP, D])

            pool.wait_ge(rows_loaded, 64)

            def turn(g, project, attend, experts):
                ahead, now, last, before = counts(pool, g)
                if not since(g, 0):
                    rstd(st1, y_var, y_rstd, 1)
                    rstd(st2, h_var, h_rstd, 1)
                elif project:
                    pool.wait_ge(y_added, ahead)
                    eng.tensor_tensor(y_g[0:ROWS], y_c[0:ROWS], row(gamma_sb[0:ROWS, :]),
                                      ALU.mult).then_inc(y_scaled, 1)
                    rstd(st1, y_var, y_rstd, ahead)
                    pool.wait_ge(y_scaled, ahead)
                    pool.wait_ge(y_rstd, ahead)
                    eng.tensor_tensor(y_n[0:ROWS], y_g[0:ROWS], wide(st1[0:ROWS, 1, :]),
                                      ALU.mult).then_inc(y_normed, 1)
                    pool.wait_ge(y_normed, ahead)
                    pool.wait_ge(h_kept, now)
                    eng.tensor_tensor(h[0:ROWS, :, 0:D], y_n[0:ROWS], row(beta_sb[0:ROWS, :]), ALU.add
                                      ).then_inc(h_ready, 1)
                    rstd(st2, h_var, h_rstd, ahead)
                    pool.wait_ge(h_rstd, ahead)
                    pool.wait_ge(s_in_psum, now)
                    pool.wait_ge(s_tok_made, now)
                    eng.tensor_tensor(s[0:ROWS, 0:GP], h_c[0:ROWS], wide(st2[0:ROWS, 1, :]),
                                      ALU.mult).then_inc(s_ready, 1)
                if attend:
                    rstd(st3, a_var, a_rstd, now)
                if attend and since(g, 1):
                    pool.wait_ge(a_ready, now)
                    eng.tensor_copy(h_of(g, D), a[0:ROWS, :, 0:D]).then_inc(a_kept, 1)

            turns(pool, turn)

        @block.scalar
        def _(act):
            eng = nc.scalar
            act.dma_start(tokw_raw[:], tok_w).then_inc(tokw_loaded, 16)
            for dst, src in ((tokb_sb, tok_b), (gamma_sb, tok_gamma), (beta_sb, tok_beta), (rb2_sb, router_b2)):
                act.dma_start(dst[:], src.partition_broadcast(128)).then_inc(rows_loaded, 16)
            act.dma_start(e_raw[:].rearrange("i (h j) -> i h j", h=HEADS),
                          attn_e.rearrange("h i j -> i h j")).then_inc(e_loaded, 16)

            def turn(g, project, attend, experts):
                ahead, now, last, before = counts(act, g)
                first = attend and not since(g, 1)
                s_ps = zb[0] if first else tb

                def qs_copy(i):
                    act.wait_ge(qs_in_psum[i], now)
                    if i == 0 and since(g, 1):
                        act.wait_ge(om_in_psum[GP - 1], last)
                    eng.copy(qs[:, :, i, :], ring[i % 2][:, 0:N].rearrange("p (c t) -> p c t", c=GC)
                             ).then_inc(qs_copied[i], 1)

                def z_copy(i):
                    act.wait_ge(z_in_psum[i], now)
                    if i == 0 and since(g, 1):
                        act.wait_ge(rt_in_psum, last)
                    eng.copy(z_t[:, :, 2 * i:2 * i + 2, :].rearrange("p h s t -> p s h t"),
                             zb[i % 2][:, 0:2 * HP * T].rearrange("p (s h t) -> p s h t", s=2, h=HP)
                             ).then_inc(z_copied[i], 1)

                def a_square(value):
                    act.wait_ge(a_centred, value)
                    eng.activation(a_sq[0:ROWS, :, 0:D], a_c[0:ROWS], ACT.Square, scale=D ** -0.5
                                   ).then_inc(a_squared, 1)

                def s_upper_copy():
                    if not since(g, 0):
                        act.wait_ge(cleared, 12)
                    act.wait_ge(s_in_psum, ahead)
                    if since(g, 0):
                        act.wait_ge(qs_in_psum[HP - 1], now)
                    eng.copy(s_split[0:64], clips_of(s_ps)[0:64]).then_inc(s_upper, 1)

                def s_feat_copies():
                    act.wait_ge(s_split_made, ahead)
                    if since(g, 0):
                        act.wait_ge(om_in_psum[GP - 1], now)
                    eng.copy(s_feat[0:64, :, 0:T], clips_of(s_ps)[0:64]).then_inc(s_feat_top, 1)
                    eng.copy(s_feat[64:128, :, 64:64 + T], clips_of(s_ps)[0:64]).then_inc(s_feat_made, 1)

                def rt_copy():
                    act.wait_ge(rt_in_psum, now)
                    if since(g, 1):
                        act.wait_ge(r_in_psum, last)
                    eng.copy(r_t[:, :, 0:T], tb[:, 0:N].rearrange("p (c t) -> p c t", c=GC)).then_inc(rt_copied, 1)

                def h1_relu(e):
                    act.wait_ge(h1_in_psum[e], last)
                    if since(g, 2):
                        act.wait_ge(h2_in_psum[e], before)
                    eng.activation(h1[:, e, :], ring[e % 2][:, 0:N], ACT.Relu,
                                   bias=b1_sb[:, e:e + 1]).then_inc(h1_made[e], 1)

                def h2_relu(e):
                    act.wait_ge(h2_in_psum[e], last)
                    if attend:
                        if since(g, 2):
                            act.wait_ge(h2_weighted[e], before)
                        dst = h2[:, e, :].rearrange("p (c t) -> p c t", c=GC)
                    else:
                        act.wait_ge(o_in_psum, before)
                        dst = h2w[:, e, :, 0:T]
                    eng.activation(dst, ring[(e + 1) % 2][:, 0:N].rearrange("p (c t) -> p c t", c=GC), ACT.Relu,
                                   bias=b2_sb[:, e:e + 1]).then_inc(h2_made[e], 1)

                def x_copy(value):
                    act.wait_ge(x_in_psum, value)
                    act.wait_ge(y_in_psum, value - 1 if isinstance(value, int) else now)
                    eng.copy(x_t[:], pairs_of(zb[1], BROWS)).then_inc(x_copied, 1)

                def h_square():
                    act.wait_ge(h_centred, ahead)
                    eng.activation(h_sq[0:ROWS, :, 0:D], h_c[0:ROWS], ACT.Square, scale=D ** -0.5
                                   ).then_inc(h_squared, 1)

                def y_square(value):
                    act.wait_ge(y_added, value)
                    eng.activation(y_sq[0:ROWS, :, 0:D], y_c[0:ROWS], ACT.Square, scale=D ** -0.5
                                   ).then_inc(y_squared, 1)

                def split_upper():
                    act.wait_ge(a_in_psum, last)
                    if since(g, 2):
                        act.wait_ge(h1_in_psum[EP - 1], before)
                    eng.copy(h_split[0:64], clips_of(tb)[0:64]).then_inc(a_upper, 1)

                if attend:
                    qs_copy(0)
                if experts and since(g, 2):
                    split_upper()
                elif experts:
                    a_square(last)
                if project and since(g, 1):
                    x_copy(ahead)
                if attend:
                    qs_copy(2)
                if first:
                    h_square()
                if experts and not since(g, 2):
                    split_upper()
                if experts:
                    act.wait_ge(rh_in_psum, last)
                    if since(g, 2):
                        act.wait_ge(l_in_psum, before)
                    if not since(g, 2):
                        act.wait_ge(rest_loaded, 15 * 16)
                    eng.activation(rh[:, :, 0:T], tb[0:RHID, 0:N].rearrange("p (c t) -> p c t", c=GC),
                                   ACT.Relu, bias=rb1_sb[:, 0:1]).then_inc(rh_made, 1)
                if experts:
                    h1_relu(0)
                    h1_relu(1)
                if project and since(g, 1):
                    y_square(ahead)
                elif not since(g, 0):
                    y_square(1)
                if not since(g, 0):
                    x_copy(2)
                if experts and attend:
                    h1_relu(2)
                if experts:
                    act.wait_ge(l_centred, last)
                    eng.activation(ex[0:ROWS], logits_c[0:ROWS], ACT.Exp).then_inc(ex_made, 1)
                if experts and not attend:
                    h1_relu(2)
                if attend:
                    z_copy(0)
                    z_copy(1)
                elif experts:
                    h2_relu(0)
                if experts:
                    act.wait_ge(probs_made, last)
                    eng.activation(ex2[0:ROWS], probs[0:ROWS], ACT.Exp).then_inc(ex2_made, 1)
                if attend:
                    z_copy(2)
                    z_copy(3)
                if experts and attend:
                    h2_relu(0)
                if project and not first:
                    h_square()
                if not since(g, 0):
                    y_square(2)
                if first:
                    s_upper_copy()
                    s_feat_copies()
                if attend:
                    rt_copy()
                if experts:
                    h2_relu(1)
                if experts and not attend:
                    h2_relu(2)
                if experts and attend:
                    act.wait_ge(gt_in_psum, last)
                    if since(g, 2):
                        act.wait_ge(o_in_psum, before)
                    eng.copy(gate_t[:].rearrange("p (a s) u -> p a (s u)", s=2)[:, :, 0:ROWS + 1],
                             pairs_of(gt_ps, ROWS + 1)).then_inc(gt_copied, 1)
                    h2_relu(2)
                if attend and not first:
                    a_square(now)
                if project and not first:
                    s_upper_copy()
                    s_feat_copies()

            turns(act, turn)

        @block.vector
        def _(dve):
            eng = nc.vector
            eng.memset(xin[:], 0.0).then_inc(xin_cleared, 1)
            dve.wait_ge(w_in_psum, 1)
            eng.tensor_copy(tokw_whole[:], yb[:, 0:2 * D].rearrange("p (h i) -> p h i", h=2)).then_inc(w_copied, 1)
            dve.wait_ge(w_copied, 1)
            eng.tensor_reduce(w_sums[:, 0:2], tokw_whole[:], axis=AX.X, op=ALU.add).then_inc(w_summed, 1)
            dve.wait_ge(w_summed, 1)
            eng.scalar_tensor_tensor(tokw_t[:], w_sums[:, 0:2].unsqueeze(2).to_broadcast([128, 2, D]), -1.0 / D,
                                     tokw_whole[:], ALU.mult, ALU.add).then_inc(w_centred, 1)
            dve.wait_ge(x_in_psum, 1)
            eng.tensor_copy(x_t[:], pairs_of(zb[1], BROWS)).then_inc(x_copied, 1)
            eng.memset(fold[:], 1.0).then_inc(fold_step, 1)
            dve.wait_ge(fold_step, 1)
            for rows in (slice(0, D), slice(D, 2 * D)):
                eng.tensor_copy(fold[rows, 0:D], ident[rows, rows]).then_inc(fold_step, 1)
            for tile in (y_sq, h_sq, a_sq):
                eng.memset(tile[:], EPS).then_inc(cleared, 1)
            dve.wait_ge(rows_loaded, 64)
            eng.tensor_reduce(w_sums[:, 2:3], tokb_sb[:].unsqueeze(1), axis=AX.X, op=ALU.add).then_inc(w_summed, 1)
            dve.wait_ge(w_summed, 2)
            eng.scalar_tensor_tensor(tokb_c[:], w_sums[:, 2:3].to_broadcast([128, D]), -1.0 / D, tokb_sb[:],
                                     ALU.mult, ALU.add).then_inc(w_centred, 1)
            dve.wait_ge(w_centred, 2)

            parts = ((q_raw, q_hi, q_lo), (w1_raw, w1_hi, w1_lo), (rw1_raw, rw1_hi, rw1_lo))

            def upper_weights(k):
                raw, hi, lo = parts[k]
                eng.tensor_copy(hi[:], raw[:]).then_inc(q_rounded, 1)

            def lower_weights(k):
                raw, hi, lo = parts[k]
                dve.wait_ge(q_rounded, k + 1)
                eng.tensor_tensor(lo[:], raw[:], hi[:].bitcast(F32), ALU.subtract).then_inc(q_split, 1)

            def split_rest():
                for k in (1, 2):
                    upper_weights(k)
                    lower_weights(k)
                dve.wait_ge(spread_made, 1)
                eng.tensor_copy(spread[:].rearrange("p e m -> p (e m)"), spread_raw[:]).then_inc(spread_rounded, 1)

            def split_b3():
                dve.wait_ge(rest_loaded, 15 * 16)
                eng.tensor_copy(b3_hi[:], b3_raw[:]).then_inc(q_rounded, 1)
                eng.tensor_copy(b3_parts[:], b3_raw[:]).then_inc(q_rounded, 1)
                eng.tensor_copy(b3_rows[:], b3_flat[:]).then_inc(q_rounded, 1)
                dve.wait_ge(q_rounded, 6)
                eng.tensor_tensor(b3_parts[32:64], b3_raw[32:64], b3_hi[32:64].bitcast(F32),
                                  ALU.subtract).then_inc(q_split, 1)
                eng.tensor_tensor(b3_rows[32:64], b3_flat[32:64], b3_rows[32:64].bitcast(F32),
                                  ALU.subtract).then_inc(q_split, 1)
                dve.wait_ge(cleared, 12)
                eng.tensor_copy(ones[:], ones_raw[:]).then_inc(q_split, 1)

            def row(v, n):
                return v.unsqueeze(1).to_broadcast([ROWS, GP, n])

            def wide(v, n):
                return v.unsqueeze(2).to_broadcast([ROWS, GP, n])

            def sum_rows(out_, in_, done):
                eng.tensor_reduce(out_, in_, axis=AX.X, op=ALU.add).then_inc(done, 1)

            def centre(out_, in_, sums, done):
                eng.scalar_tensor_tensor(out_, wide(sums, D), -1.0 / D, in_, ALU.mult, ALU.add).then_inc(done, 1)

            def turn(g, project, attend, experts):
                ahead, now, last, before = counts(dve, g)
                first = attend and not since(g, 1)
                s_ps = zb[0] if first else tb

                def mask(i):
                    dve.wait_ge(om_in_psum[i], now)
                    if since(g, 1):
                        dve.wait_ge(z_in_psum[i], last)
                    eng.tensor_tensor(omega[0:ROWS, 2 * i:2 * i + 2, :, :].rearrange("p c h t -> p (c h t)"),
                                      om[i % 2][0:ROWS, 0:N], causal[0:ROWS, :], ALU.mult).then_inc(om_masked[i], 1)

                def weigh(e):
                    dve.wait_ge(h2_made[e], last)
                    dve.wait_ge(gate_in_psum[e], last)
                    if e == 0 and since(g, 2):
                        dve.wait_ge(o_in_psum, before)
                    eng.tensor_tensor(h2w[:, e, :, 0:T], gates_of(gates[e]),
                                      h2[:, e, :].rearrange("p (c t) -> p c t", c=GC),
                                      ALU.mult).then_inc(h2_weighted[e], 1)

                def split_s():
                    dve.wait_ge(s_upper, ahead)
                    eng.tensor_tensor(s_split[64:128], clips_of(s_ps)[0:64], s_split[0:64].bitcast(F32),
                                      ALU.subtract).then_inc(s_split_made, 1)

                def a_variance(value):
                    dve.wait_ge(a_squared, value)
                    sum_rows(st3[0:ROWS, 0, :], a_sq[0:ROWS], a_var)

                def keep_a(group):
                    eng.tensor_copy(h_of(group, D), a[0:ROWS, :, 0:D]).then_inc(a_kept, 1)

                def normalise_a(value):
                    dve.wait_ge(a_rstd, value)
                    eng.tensor_tensor(a_n[0:ROWS, 0:GP], a_c[0:ROWS], wide(st3[0:ROWS, 1, :], D),
                                      ALU.mult).then_inc(a_normed, 1)

                def s_tok_copies(group_after):
                    dve.wait_ge(s_ready, ahead if group_after else now)
                    if since(g, 0):
                        dve.wait_ge(z_in_psum[GP - 1], now if group_after else last)
                    for side in range(2):
                        for par in range(2):
                            last_copy = eng.tensor_copy(
                                s_tok[64 * par:64 * par + T, :, 64 * par:64 * par + D].rearrange(
                                    "p (a c) d -> p a c d", c=2)[:, :, side, :],
                                s[64 * side:64 * side + T, 0:GP, :])
                    last_copy.then_inc(s_tok_made, 1)

                def qs_copy(i):
                    dve.wait_ge(qs_in_psum[i], now)
                    if i == 1 and since(g, 1):
                        dve.wait_ge(om_in_psum[GP - 1], last)
                    eng.tensor_copy(qs[:, :, i, :], ring[i % 2][:, 0:N].rearrange("p (c t) -> p c t", c=GC)
                                    ).then_inc(qs_copied[i], 1)

                def y_add(value):
                    dve.wait_ge(y_in_psum, value)
                    if not (isinstance(value, int) and value == 1):
                        dve.wait_ge(y_scaled, value - 1 if isinstance(value, int) else now)
                    eng.tensor_tensor(y_c[0:ROWS], y_ps[0:ROWS], row(tokb_c[0:ROWS, :], D),
                                      ALU.add).then_inc(y_added, 1)

                def h_sums():
                    dve.wait_ge(h_ready, ahead)
                    sum_rows(h[0:ROWS, :, D], h[0:ROWS, :, 0:D], h_summed)

                def centre_h():
                    dve.wait_ge(h_summed, ahead)
                    if since(g, 0):
                        dve.wait_ge(s_ready, now)
                    centre(h_c[0:ROWS], h[0:ROWS, :, 0:D], h[0:ROWS, :, D], h_centred)
                    eng.tensor_copy(h_of(g + 1), h[0:ROWS]).then_inc(h_kept, 1)

                def h_variance():
                    dve.wait_ge(h_squared, ahead)
                    sum_rows(st2[0:ROWS, 0, :], h_sq[0:ROWS], h_var)

                def y_variance(value):
                    dve.wait_ge(y_squared, value)
                    sum_rows(st1[0:ROWS, 0, :], y_sq[0:ROWS], y_var)

                def split_lower():
                    dve.wait_ge(a_upper, last)
                    eng.tensor_tensor(h_split[64:128], clips_of(tb)[0:64], h_split[0:64].bitcast(F32),
                                      ALU.subtract).then_inc(a_split_made, 1)

                if attend:
                    qs_copy(1)
                if experts and since(g, 2):
                    split_lower()
                elif experts:
                    a_variance(last)
                if attend:
                    qs_copy(3)
                if experts and not since(g, 2):
                    keep_a(g - 1)
                    normalise_a(last)
                if first:
                    h_sums()
                    centre_h()
                    h_variance()
                if attend and since(g, 2):
                    s_tok_copies(False)
                if project and since(g, 1):
                    y_add(ahead)
                elif not since(g, 0):
                    y_add(1)
                if experts and not since(g, 2):
                    split_lower()
                    split_b3()
                if not since(g, 0):
                    dve.wait_ge(y_added, 1)
                    eng.tensor_tensor(y_g[0:ROWS], y_c[0:ROWS], row(gamma_sb[0:ROWS, :], D),
                                      ALU.mult).then_inc(y_scaled, 1)
                if attend:
                    mask(0)
                if experts:
                    dve.wait_ge(l_in_psum, last)
                    eng.tensor_tensor(logits[0:ROWS], l_ps[0:ROWS], row(rb2_sb[0:ROWS, :], EXPERTS),
                                      ALU.add).then_inc(l_added, 1)
                    dve.wait_ge(l_added, last)
                    eng.tensor_reduce(rst[0:ROWS, 0, :], logits[0:ROWS], axis=AX.X, op=ALU.max).then_inc(l_max, 1)
                if project and since(g, 1):
                    y_variance(ahead)
                elif not since(g, 0):
                    y_variance(1)
                if experts:
                    dve.wait_ge(l_max, last)
                    eng.tensor_tensor(logits_c[0:ROWS], logits[0:ROWS], wide(rst[0:ROWS, 0, :], EXPERTS),
                                      ALU.subtract).then_inc(l_centred, 1)
                if not since(g, 0):
                    for tile in (s, s_feat):
                        eng.memset(tile[:], 0.0).then_inc(cleared, 1)
                    dve.wait_ge(y_rstd, 1)
                    eng.tensor_tensor(y_n[0:ROWS], y_g[0:ROWS], wide(st1[0:ROWS, 1, :], D),
                                      ALU.mult).then_inc(y_normed, 1)
                    dve.wait_ge(y_normed, 1)
                    eng.tensor_tensor(h[0:ROWS, :, 0:D], y_n[0:ROWS], row(beta_sb[0:ROWS, :], D),
                                      ALU.add).then_inc(h_ready, 1)
                if attend:
                    mask(1)
                if experts:
                    dve.wait_ge(ex_made, last)
                    sum_rows(rst[0:ROWS, 1, :], ex[0:ROWS], ex_summed)
                    dve.wait_ge(ex_summed, last)
                    eng.reciprocal(rst[0:ROWS, 2, :], rst[0:ROWS, 1, :]).then_inc(ex_inv, 1)
                    dve.wait_ge(ex_inv, last)
                    eng.tensor_tensor(probs[0:ROWS], ex[0:ROWS], wide(rst[0:ROWS, 2, :], EXPERTS),
                                      ALU.mult).then_inc(probs_made, 1)
                if attend:
                    mask(2)
                if experts:
                    shape = [ROWS, GP, EXPERTS, EXPERTS]
                    other = probs[0:ROWS].unsqueeze(2).to_broadcast(shape)
                    own = probs[0:ROWS].unsqueeze(3).to_broadcast(shape)
                    dve.wait_ge(probs_made, last)
                    eng.tensor_tensor(above[0:ROWS], other, own, ALU.is_gt).then_inc(above_made, 1)
                    eng.tensor_tensor(tied[0:ROWS], other, own, ALU.is_ge).then_inc(tied_made, 1)
                if attend:
                    mask(3)
                if first:
                    split_rest()
                    split_s()
                    s_tok_copies(True)
                if experts:
                    dve.wait_ge(tied_made, last)
                    eng.tensor_tensor(tied_e[0:ROWS], tied[0:ROWS],
                                      earlier[0:ROWS].unsqueeze(1).to_broadcast(shape), ALU.mult).then_inc(tied_cut, 1)
                    dve.wait_ge(above_made, last)
                    dve.wait_ge(tied_cut, last)
                    eng.tensor_tensor(beats[0:ROWS], above[0:ROWS], tied_e[0:ROWS], ALU.max).then_inc(beats_made, 1)
                    dve.wait_ge(beats_made, last)
                    eng.tensor_reduce(rank[0:ROWS], beats[0:ROWS], axis=AX.X, op=ALU.add).then_inc(rank_made, 1)
                    dve.wait_ge(rank_made, last)
                    dve.wait_ge(ex2_made, last)
                    eng.scalar_tensor_tensor(picked[0:ROWS], rank[0:ROWS], 1.5, ex2[0:ROWS], ALU.is_lt,
                                             ALU.mult).then_inc(picked_made, 1)
                    dve.wait_ge(picked_made, last)
                    sum_rows(rst[0:ROWS, 3, :], picked[0:ROWS], picked_sum)
                if project and not first:
                    h_sums()
                if experts:
                    dve.wait_ge(picked_sum, last)
                    eng.reciprocal(rst[0:ROWS, 4, :], rst[0:ROWS, 3, :]).then_inc(picked_inv, 1)
                if project and not first:
                    centre_h()
                if experts:
                    dve.wait_ge(picked_inv, last)
                    eng.tensor_tensor(gate[0:ROWS], picked[0:ROWS], wide(rst[0:ROWS, 4, :], EXPERTS),
                                      ALU.mult).then_inc(gate_made, 1)
                    dve.wait_ge(gate_made, last)
                if experts and attend:
                    if since(g, 2):
                        dve.wait_ge(gt_in_psum, before)
                    twice = gate[0:ROWS].unsqueeze(2).to_broadcast([ROWS, GP, 2, EXPERTS])
                    eng.tensor_copy(gate_up.bitcast(F32R), twice).then_inc(gate_upper, 1)
                    dve.wait_ge(gate_upper, last)
                    eng.tensor_tensor(gate_low, twice, gate_up, ALU.subtract).then_inc(gate_split, 1)
                if project and not first:
                    h_variance()
                if not since(g, 0):
                    y_add(2)
                    dve.wait_ge(q_loaded, 6 * 16)
                    upper_weights(0)
                    y_variance(2)
                    dve.wait_ge(h_rstd, 1)
                    eng.tensor_tensor(s[0:ROWS, 0:GP], h_c[0:ROWS], wide(st2[0:ROWS, 1, :], D),
                                      ALU.mult).then_inc(s_ready, 1)
                    lower_weights(0)
                    dve.wait_ge(e_in_psum, 1)
                    eng.tensor_copy(e_t[:], ring[0][:, 0:HP * D].rearrange("p (h i) -> p h i", h=HP)).then_inc(e_copied, 1)
                if attend:
                    dve.wait_ge(r_in_psum, now)
                    dve.wait_ge(h_kept, now)
                    if since(g, 2):
                        dve.wait_ge(a_kept, last)
                    eng.tensor_tensor(a[0:ROWS], r_ps[0:ROWS], h_of(g), ALU.add).then_inc(a_ready, 1)
                if experts and project:
                    weigh(0)
                if attend:
                    dve.wait_ge(a_ready, now)
                    centre(a_c[0:ROWS], a[0:ROWS, :, 0:D], a[0:ROWS, :, D], a_centred)
                if experts and attend:
                    weigh(1 if project else 0)
                if attend and not first:
                    a_variance(now)
                if experts and attend:
                    if not project:
                        weigh(1)
                    weigh(2)
                if project and since(g, 1):
                    split_s()
                if attend and not first:
                    if since(g, 1):
                        dve.wait_ge(a_in_psum, last)
                    normalise_a(now)
                if project and not first:
                    if not since(g, 0):
                        split_s()
                        s_tok_copies(True)
                if not since(g, 0):
                    dve.wait_ge(half_mask, 1)
                    eng.tensor_copy(causal[64:128, :], causal[0:64, :]).then_inc(mask_made, 1)
                if experts and not attend:
                    for e in range(EP):
                        dve.wait_ge(outs_in_psum[e], 1)
                        pair_gates = gate[0:ROWS, :, 2 * e:2 * e + 2].unsqueeze(3).to_broadcast([ROWS, GP, 2, D])
                        eng.tensor_tensor(outs[0:ROWS, e].rearrange("p a (s d) -> p a s d", s=2),
                                          gates[e][0:ROWS, :].rearrange("p (a s d) -> p a s d", a=GP, s=2),
                                          pair_gates, ALU.mult).then_inc(outs_weighted, 1)
                        if e >= 1:
                            dve.wait_ge(outs_weighted, 2 * e)
                            eng.tensor_tensor(outs[0:ROWS, 0], outs[0:ROWS, 0], outs[0:ROWS, e],
                                              ALU.add).then_inc(outs_weighted, 1)
                    dve.wait_ge(outs_weighted, 5)
                    eng.tensor_tensor(outs[0:ROWS, 1, :, 0:D], outs[0:ROWS, 0, :, 0:D], outs[0:ROWS, 0, :, D:2 * D],
                                      ALU.add).then_inc(outs_weighted, 1)
                    dve.wait_ge(outs_weighted, 6)
                    dve.wait_ge(a_kept, last)
                    eng.tensor_tensor(h_of(g - 1, D), outs[0:ROWS, 1, :, 0:D], h_of(g - 1, D),
                                      ALU.add).then_inc(o_added, 1)
                elif experts:
                    dve.wait_ge(o_in_psum, last)
                    dve.wait_ge(a_kept, last)
                    eng.tensor_tensor(h_of(g - 1, D), o_ps[0:ROWS], h_of(g - 1, D), ALU.add).then_inc(o_added, 1)

            turns(dve, turn)

        @block.tensor
        def _(pe):
            mm, tr = nc.tensor.matmul, nc.tensor.transpose

            def keep_clock(times, bank):
                for _ in range(times):
                    mm(bank[:, 0:128], ident[:], ident[:], start=True, stop=True)

            pe.wait_ge(consts, 1)
            pe.wait_ge(tokw_loaded, 16)
            for half in range(2):
                done = tr(yb[0:128, D * half:D * (half + 1)], tokw_raw[:, BLK * half:BLK * (half + 1)],
                          ident[0:D, 0:D])
            done.then_inc(w_in_psum, 1)

            def split_matmul(out_, hi, lo, moving):
                mm(out_, hi, moving, start=True, stop=False)
                return mm(out_, lo, moving, start=False, stop=True)

            def turn(g, project, attend, experts):
                ahead, now, last, before = counts(pe, g)
                first = attend and not since(g, 1)
                s_ps = zb[0] if first else tb

                def qs_product(i):
                    if i == 0:
                        pe.wait_ge(s_split_made, now)
                        if since(g, 1):
                            pe.wait_ge(h2_made[EP - 1], before)
                    if i >= 2:
                        pe.wait_ge(qs_copied[i - 2], now)
                    split_matmul(ring[i % 2][:, 0:N], q_hi[:, i, :], q_lo[:, i, :],
                                 s_split[:].rearrange("p c t -> p (c t)")).then_inc(qs_in_psum[i], 1)

                def omega_product(i):
                    if i == 0:
                        pe.wait_ge(qs_copied[HP - 2], now)
                        pe.wait_ge(qs_copied[HP - 1], now)
                        pe.wait_ge(s_feat_made, now)
                    if i >= 2:
                        pe.wait_ge(om_masked[i - 2], now)
                    elif since(g, 1):
                        pe.wait_ge(om_masked[i + 2], last)
                    if i == 0 and project:
                        pe.wait_ge(y_added, ahead)
                    elif i == 0:
                        pe.wait_ge(h2_weighted[2], before)
                    if i == 1 and since(g, 2):
                        pe.wait_ge(gt_copied, before)
                    for c in range(2):
                        done = mm(om[i % 2][0:ROWS, HP * T * c:HP * T * (c + 1)], s_feat[:, 2 * i + c, 0:ROWS],
                                  qs[:, 2 * i + c, :, :].rearrange("p h t -> p (h t)"), start=True, stop=True)
                    done.then_inc(om_in_psum[i], 1)

                def z_product(i):
                    pe.wait_ge(om_masked[i], now)
                    if i == 0:
                        pe.wait_ge(s_tok_made, now)
                        if since(g, 2):
                            pe.wait_ge(h2_weighted[0], before)
                    elif i == 1 and project:
                        pe.wait_ge(x_copied, ahead)
                    elif i == 1:
                        pe.wait_ge(h2_weighted[1], before)
                    elif i >= 2:
                        pe.wait_ge(z_copied[i - 2], now)
                    for c in range(2):
                        done = mm(zb[i % 2][:, HP * T * c:HP * T * (c + 1)], s_tok[0:ROWS, 2 * i + c, :],
                                  omega[0:ROWS, 2 * i + c, :, :].rearrange("p h t -> p (h t)"), start=True, stop=True)
                    done.then_inc(z_in_psum[i], 1)

                def gate_spread(e):
                    if e == 0:
                        pe.wait_ge(gt_copied, last)
                    if e == 2:
                        pe.wait_ge(om_masked[2], now)
                    else:
                        pe.wait_ge(z_copied[2 + e], now)
                    mm(gates[e][:, 0:GC * (T + 1)], spread[:, e, :], gate_t[:, :, 0:T + 1],
                       start=True, stop=True).then_inc(gate_in_psum[e], 1)

                def h1_product(e):
                    if e == 2:
                        pe.wait_ge(h1_made[0], last)
                    elif attend:
                        pe.wait_ge(qs_copied[2 + e], now)
                    elif e == 0:
                        pe.wait_ge(h2_made[EP - 1], before)
                    split_matmul(ring[e % 2][:, 0:N], w1_hi[:, e, :], w1_lo[:, e, :],
                                 h_split[:].rearrange("p c t -> p (c t)")).then_inc(h1_in_psum[e], 1)

                def head_sums():
                    pe.wait_ge(z_copied[GP - 1], now)
                    if experts:
                        pe.wait_ge(rh_made, last)
                    else:
                        pe.wait_ge(s_feat_made, now)
                    for i in range(HP):
                        side = 64 * (i % 2)
                        done = mm(tb[side:side + 64, 0:N], e_t[:, i, :],
                                  z_t[:, i, :, :].rearrange("p c t -> p (c t)"), start=i < 2, stop=i >= 2)
                    done.then_inc(rt_in_psum, 1)

                def fold_heads():
                    pe.wait_ge(rt_copied, now)
                    if experts:
                        pe.wait_ge(l_added, last)
                    for p in range(GP):
                        done = mm(yb[0:ROWS, (D + 1) * p:(D + 1) * (p + 1)],
                                  r_t[:, 2 * p:2 * p + 2, :].rearrange("p c u -> p (c u)")[:, 0:ROWS], fold[:],
                                  start=True, stop=True)
                    done.then_inc(r_in_psum, 1)

                def s_transposes():
                    pe.wait_ge(s_ready, ahead)
                    if first:
                        pe.wait_ge(z_copied[2], now)
                    elif attend:
                        pe.wait_ge(rt_copied, now)
                    for p in range(GP):
                        done = tr(s_ps[:, 128 * p:128 * p + ROWS],
                                  s[0:ROWS, p:p + 2, :].rearrange("p a d -> p (a d)"), ident[0:ROWS, 0:ROWS])
                    done.then_inc(s_in_psum, 1)

                def last_layer(e):
                    pe.wait_ge(h2_weighted[e], last)
                    for p in range(GP):
                        done = mm(yb[0:ROWS, D * p:D * (p + 1)],
                                  h2w[:, e, 2 * p:2 * p + 2, :].rearrange("p c u -> p (c u)")[:, 0:ROWS],
                                  w3_sb[:, e, :], start=False, stop=e == EP - 1,
                                  skip_group_check=True)
                    return done

                def h2_product(e):
                    pe.wait_ge(h1_made[e], last)
                    if e < 2:
                        pe.wait_ge(h1_made[e + 1], last)
                    else:
                        pe.wait_ge(h2_made[0], last)
                    mm(ring[(e + 1) % 2][:, 0:N], w2_diag[:, e, :], h1[:, e, :], start=True,
                       stop=True).then_inc(h2_in_psum[e], 1)

                def x_transposes(value):
                    pe.wait_ge(x_loaded, 32 * value)
                    for p in range(GP):
                        done = tr(zb[1][:, 128 * p:128 * p + BROWS], xin[0:BROWS, p, :], ident[0:BROWS, 0:BROWS])
                    done.then_inc(x_in_psum, 1)

                def y_products(value):
                    pe.wait_ge(x_copied, value)
                    for p in range(GP):
                        for half in range(2):
                            done = mm(om[0][0:ROWS, D * p:D * (p + 1)], x_t[:, p, half:half + ROWS],
                                      tokw_t[:, half, :], start=half == 0, stop=half == 1)
                    done.then_inc(y_in_psum, 1)

                if attend:
                    if not since(g, 1):
                        keep_clock(4, yb)
                        pe.wait_ge(e_copied, 1)
                        pe.wait_ge(q_split, 1)
                        pe.wait_ge(fold_step, 3)
                def h_transposes():
                    pe.wait_ge(a_normed, last)
                    if attend:
                        pe.wait_ge(s_feat_made, now)
                        pe.wait_ge(s_split_made, now)
                        if not since(g, 2):
                            pe.wait_ge(rt_copied, last)
                    else:
                        pe.wait_ge(rt_copied, last)
                    for p in range(GP):
                        done = tr(tb[:, 128 * p:128 * p + ROWS],
                                  a_n[0:ROWS, p:p + 2, :].rearrange("p a d -> p (a d)"), ident[0:ROWS, 0:ROWS])
                    done.then_inc(a_in_psum, 1)

                if attend:
                    qs_product(0)
                    qs_product(1)
                if experts and since(g, 2):
                    h_transposes()
                if project and since(g, 1):
                    if since(g, 2):
                        pe.wait_ge(h2_weighted[1], before)
                    else:
                        pe.wait_ge(z_copied[GP - 1], last)
                    x_transposes(ahead)
                elif not since(g, 0):
                    x_transposes(1)
                if attend:
                    qs_product(2)
                    qs_product(3)
                if project and since(g, 1):
                    if since(g, 2):
                        pe.wait_ge(h2_weighted[2], before)
                    else:
                        pe.wait_ge(om_masked[2], last)
                    y_products(ahead)
                if experts and not since(g, 2):
                    h_transposes()
                if experts:
                    if not attend:
                        keep_clock(3, zb[1])
                    if not since(g, 2):
                        pe.wait_ge(q_split, 3)
                        pe.wait_ge(spread_rounded, 1)
                    pe.wait_ge(a_split_made, last)
                    split_matmul(tb[0:RHID, 0:N], rw1_hi[:], rw1_lo[:],
                                 h_split[:].rearrange("p c t -> p (c t)")).then_inc(rh_in_psum, 1)
                    h1_product(0)
                    h1_product(1)
                if not since(g, 0):
                    pe.wait_ge(w_centred, 1)
                    y_products(1)
                    pe.wait_ge(e_loaded, 16)
                    for i in range(HP):
                        done = tr(ring[0][:, D * i:D * (i + 1)], e_raw[:, 128 * i:128 * (i + 1)], ident[0:D, 0:D])
                    done.then_inc(e_in_psum, 1)
                    x_transposes(2)
                    pe.wait_ge(y_added, 1)
                    y_products(2)
                if first:
                    keep_clock(1, yb)
                if attend:
                    omega_product(0)
                if experts:
                    pe.wait_ge(rh_made, last)
                    if since(g, 2):
                        pe.wait_ge(o_added, before)
                    else:
                        pe.wait_ge(a_ready, last)
                    for p in range(GP):
                        done = mm(yb[0:ROWS, EXPERTS * p:EXPERTS * (p + 1)],
                                  rh[:, 2 * p:2 * p + 2, :].rearrange("p c u -> p (c u)")[:, 0:ROWS], rw2_sb[:],
                                  start=True, stop=True)
                    done.then_inc(l_in_psum, 1)
                if attend:
                    omega_product(1)
                    if first:
                        keep_clock(2, ring[0])
                if experts:
                    h1_product(2)
                if attend:
                    z_product(0)
                    omega_product(2)
                    z_product(1)
                    omega_product(3)
                    z_product(2)
                    if experts:
                        h2_product(0)
                    z_product(3)
                    if experts:
                        h2_product(1)
                    if first:
                        s_transposes()
                    head_sums()
                    if first:
                        keep_clock(2, ring[0])
                    if experts:
                        h2_product(2)
                        pe.wait_ge(gate_split, last)
                        pe.wait_ge(om_masked[3], now)
                        for p in range(GP):
                            done = tr(gt_ps[:, 128 * p:128 * p + ROWS + 1], gate_parts[0:ROWS + 1, p, :],
                                      ident[0:ROWS + 1, 0:ROWS + 1])
                        done.then_inc(gt_in_psum, 1)
                else:
                    if experts:
                        h2_product(0)
                        h2_product(1)
                        h2_product(2)
                        for e in range(EP):
                            pe.wait_ge(h2_weighted[e], before)
                            mm(gates[e][0:ROWS, :], ones[:, 0:ROWS],
                               b3_rows[:, 2 * D * e:2 * D * (e + 1)].unsqueeze(1).to_broadcast([64, GP, 2 * D]),
                               start=True, stop=True)
                            pe.wait_ge(h2_made[e], last)
                            for p in range(GP):
                                done = mm(gates[e][0:ROWS, 2 * D * p:2 * D * (p + 1)],
                                          h2w[:, e, 2 * p:2 * p + 2, :].rearrange("p c u -> p (c u)")[:, 0:ROWS],
                                          w3_diag[:, e, :, :].rearrange("p s d -> p (s d)"), start=False, stop=True,
                                          skip_group_check=True)
                            done.then_inc(outs_in_psum[e], 1)
                if attend:
                    fold_heads()
                if experts and attend:
                    for e in range(EP):
                        gate_spread(e)
                if not since(g, 0):
                    keep_clock(8, yb)
                if project and not first:
                    s_transposes()
                if experts and attend:
                    if not since(g, 2):
                        pe.wait_ge(q_split, 6)
                    pe.wait_ge(a_ready, now)
                    for p in range(GP):
                        mm(yb[0:ROWS, D * p:D * (p + 1)],
                           gate_t[:, 2 * p:2 * p + 2, :].rearrange("p c u -> p (c u)")[:, 0:ROWS], b3_parts[:],
                           start=p == 0, stop=False, skip_group_check=True)
                    last_layer(0)
                    last_layer(1)
                    last_layer(2).then_inc(o_in_psum, 1)

            turns(pe, turn)


_INS = ['x', 'L0_tok_W', 'L0_tok_b', 'L0_tok_gamma', 'L0_tok_beta', 'L0_attn_Q', 'L0_attn_E',
        'L0_ffn_router_w1', 'L0_ffn_router_b1', 'L0_ffn_router_w2', 'L0_ffn_router_b2',
        'L0_ffn_expert_w1', 'L0_ffn_expert_b1', 'L0_ffn_expert_w2', 'L0_ffn_expert_b2',
        'L0_ffn_expert_w3', 'L0_ffn_expert_b3']
_OUTS = [((64, 45, 64), 'float32')]


def kernel(**inputs):
    import numpy as _np
    import concourse.bacc as _bacc
    from concourse import mybir as _mybir
    from concourse.bass_utils import run_bass_kernel_spmd as _run

    nc = _bacc.Bacc("TRN2", target_bir_lowering=False, num_devices=1)
    arrays, args = {}, []
    for name in _INS:
        a = _np.ascontiguousarray(inputs[name])
        arrays[f"in_{name}_dram"] = a
        args.append(nc.dram_tensor(f"in_{name}_dram", a.shape, _mybir.dt.from_np(a.dtype), kind="ExternalInput").ap())
    for i, (shape, dtype) in enumerate(_OUTS):
        dt = _mybir.dt.from_np(_np.dtype(dtype))
        args.append(nc.dram_tensor(f"out_{i}_dram", shape, dt, kind="ExternalOutput").ap())
    audio_tower(nc, *args)
    r = _run(nc, [arrays], core_ids=[0])
    got = tuple(r.results[0][f"out_{i}_dram"] for i in range(len(_OUTS)))
    return got[0]
```
